# Optimizing a Trainium2 kernel written in Bass

```python
import numpy as np
import jax
import jax.numpy as jnp

def _softmax(x, axis=-1):
    return jax.nn.softmax(x, axis=axis)

def _gelu(x):
    return jax.nn.gelu(x, approximate=True)

def _silu(x):
    return jax.nn.silu(x)

def _sigmoid(x):
    return jax.nn.sigmoid(x)

def _layernorm(x, axis=-1, eps=1e-05):
    m = jnp.mean(x, axis=axis, keepdims=True)
    v = jnp.var(x, axis=axis, keepdims=True)
    return (x - m) / jnp.sqrt(v + eps)

def _scatter_add(tgt, idx, src, axis=0):
    return tgt.at[idx].add(src)

def _segment_sum(src, seg, n):
    return jax.ops.segment_sum(src, seg, n)
kernel_name = 'mk_decoder_postln_d1_seqx_r8_da0a43'

def setup_inputs(seed: int=0):
    np.random.seed(seed)
    _w = jnp.asarray

    def _rec_inputs():
        import jax
        import jax.numpy as jnp
        _rk = jax.random.key(seed)
        x = -4.161e-06 + 1 * jax.random.normal(jax.random.fold_in(_rk, 1), (16, 128, 256), jnp.float32)
        _lenS = 128 - jax.random.randint(jax.random.fold_in(_rk, 7), (16,), 0, max(1, 128 // 4) + 1, jnp.int32)
        _lenS2 = 128 - jax.random.randint(jax.random.fold_in(_rk, 8), (16,), 0, max(1, 128 // 4) + 1, jnp.int32)
        _ctx_2048P = jax.random.normal(jax.random.fold_in(_rk, 11), (16, 16, 256), jnp.float32)
        _ctx_2048c = jax.random.dirichlet(jax.random.fold_in(_rk, 511), 0.3 * jnp.ones((16,), jnp.float32), (16, 128))
        _ctx_2048t = jnp.einsum('bsk,bkd->bsd', _ctx_2048c, _ctx_2048P)
        _ctx_2048t = _ctx_2048t * jax.lax.rsqrt(jnp.mean(jnp.square(_ctx_2048t)) + 1e-12) * 0.953939
        ctx_2048 = -0.000192764 + 0.999654 * (_ctx_2048t + 0.3 * jax.random.normal(jax.random.fold_in(_rk, 611), (16, 128, 256), jnp.float32))
        return (x, ctx_2048)
    x, ctx_2048 = _rec_inputs()

    def _L0_attn_setup():
        import jax, jax.numpy as jnp
        import numpy as np
        B, T, D = (2, 256, 256)
        HQ, HKV = (32, 8)
        HD = D // HQ
        G = HQ // HKV
        ROPE_BASE = 10000.0

        def _rope(q, k):
            t, d = (q.shape[2], q.shape[3])
            inv_freq = 1.0 / ROPE_BASE ** (jnp.arange(0, d, 2, dtype=jnp.float32) / d)
            ang = jnp.arange(t, dtype=jnp.float32)[:, None] * inv_freq[None, :]
            cos = jnp.concatenate([jnp.cos(ang), jnp.cos(ang)], axis=-1)[None, None]
            sin = jnp.concatenate([jnp.sin(ang), jnp.sin(ang)], axis=-1)[None, None]

            def rot_half(x):
                x1, x2 = jnp.split(x, 2, axis=-1)
                return jnp.concatenate([-x2, x1], axis=-1)
            return (q * cos + rot_half(q) * sin, k * cos + rot_half(k) * sin)
        key = jax.random.key(seed)
        ks = jax.random.split(key, 5)
        s = 0.02
        x = jax.random.normal(ks[0], (B, T, D), dtype=jnp.float32)
        Wq = jax.random.normal(ks[1], (D, D), dtype=jnp.float32) * s
        Wk = jax.random.normal(ks[2], (HKV * HD, D), dtype=jnp.float32) * s
        Wv = jax.random.normal(ks[3], (HKV * HD, D), dtype=jnp.float32) * s
        Wo = jax.random.normal(ks[4], (D, D), dtype=jnp.float32) * s
        return {'x': x, 'Wq': Wq, 'bq': jnp.zeros((D,), jnp.float32), 'Wk': Wk, 'bk': jnp.zeros((HKV * HD,), jnp.float32), 'Wv': Wv, 'bv': jnp.zeros((HKV * HD,), jnp.float32), 'Wo': Wo, 'bo': jnp.zeros((D,), jnp.float32)}
    _L0_attn_all = _L0_attn_setup()
    _L0_attn_in = {k: v for k, v in _L0_attn_all.items() if k in ('Wq', 'bq', 'Wk', 'bk', 'Wv', 'bv', 'Wo', 'bo')}
    del _L0_attn_all

    def _L0_xattn_setup():
        import jax, jax.numpy as jnp
        import numpy as np
        FP8_MAX = 448.0
        EPS = 1e-05

        def _fp8_roundtrip(x):
            return x.astype(jnp.float8_e4m3fn).astype(jnp.float32)

        def _div_clamp_fp8(x, scale):
            y = jnp.clip(x.astype(jnp.float32) / scale, -FP8_MAX, FP8_MAX)
            y = y.astype(jnp.bfloat16).astype(jnp.float32)
            return _fp8_roundtrip(y)

        def _ln(x, w, b):
            mu = jnp.mean(x, axis=-1, keepdims=True)
            var = jnp.mean(jnp.square(x - mu), axis=-1, keepdims=True)
            return (x - mu) * jax.lax.rsqrt(var + EPS) * w + b

        def _fp8_linear_pertensor(x, wq, w_scale, in_scale):
            xq = _div_clamp_fp8(x, in_scale)
            return jnp.einsum('bsi,oi->bso', xq * in_scale, wq) * w_scale

        def _gqa(q, k, v):
            scale = 1.0 / np.sqrt(q.shape[-1])
            scores = jnp.einsum('bsghd,btgd->bghst', q, k) * scale
            p = jax.nn.softmax(scores, axis=-1)
            return jnp.einsum('bghst,btgd->bsghd', p, v)
        key = jax.random.key(seed)
        ks = jax.random.split(key, 8)
        B, S, SC, H, NH, G, D = (2, 256, 64, 256, 16, 8, 128)

        def qw(k, out_f, in_f):
            w = jax.random.normal(k, (out_f, in_f), jnp.float32) * 0.02
            sc = jnp.max(jnp.abs(w)) / FP8_MAX
            return (_fp8_roundtrip(w / sc), sc.astype(jnp.float32))
        wq, wq_s = qw(ks[0], NH * D, H)
        wqx, wqx_s = qw(ks[1], NH * D, H)
        wk, wk_s = qw(ks[2], G * D, H)
        wv, wv_s = qw(ks[3], G * D, H)
        wproj, wp_s = qw(ks[4], H, 2 * NH * D)
        return {'hidden_states': jax.random.normal(ks[5], (B, S, H), jnp.float32), 'cond': jax.random.normal(ks[6], (B, SC, H), jnp.float32), 'ln_w': jnp.ones((H,), jnp.float32), 'ln_b': jnp.zeros((H,), jnp.float32), 'wq': wq, 'wq_scale': wq_s, 'q_in_scale': jnp.full((H,), 0.05, jnp.float32), 'wqx': wqx, 'wqx_scale': wqx_s, 'qx_in_scale': jnp.full((H,), 0.05, jnp.float32), 'wk': wk, 'wk_scale': wk_s, 'k_in_scale': jnp.full((H,), 0.05, jnp.float32), 'wv': wv, 'wv_scale': wv_s, 'v_in_scale': jnp.full((H,), 0.05, jnp.float32), 'w_kv_x': jax.random.normal(ks[7], (2 * G * D, H), jnp.float32) * 0.02, 'qln_w': jnp.ones((D,), jnp.float32), 'qln_b': jnp.zeros((D,), jnp.float32), 'kln_w': jnp.ones((D,), jnp.float32), 'kln_b': jnp.zeros((D,), jnp.float32), 'qxln_w': jnp.ones((D,), jnp.float32), 'qxln_b': jnp.zeros((D,), jnp.float32), 'kxln_w': jnp.ones((D,), jnp.float32), 'kxln_b': jnp.zeros((D,), jnp.float32), 'wproj': wproj, 'proj_w_scale': wp_s, 'proj_in_scale': jnp.asarray(0.05, jnp.float32), 'proj_smooth': jnp.full((2 * NH * D,), 0.05, jnp.float32)}
    _L0_xattn_all = _L0_xattn_setup()
    _L0_xattn_in = {k: v for k, v in _L0_xattn_all.items() if k in ('ln_w', 'ln_b', 'wq', 'wq_scale', 'q_in_scale', 'wqx', 'wqx_scale', 'qx_in_scale', 'wk', 'wk_scale', 'k_in_scale', 'wv', 'wv_scale', 'v_in_scale', 'w_kv_x', 'qln_w', 'qln_b', 'kln_w', 'kln_b', 'qxln_w', 'qxln_b', 'kxln_w', 'kxln_b', 'wproj', 'proj_w_scale', 'proj_in_scale', 'proj_smooth')}
    del _L0_xattn_all

    def _L0_ffn_setup():
        import jax, jax.numpy as jnp
        import numpy as np
        HIDDEN = 256
        NUM_EXPERTS = 32
        TOP_K = 4
        MOE_INTER = 96
        GROUP = 2
        NUM_CHUNK = NUM_EXPERTS // GROUP
        CHUNK_INTER = 128
        SMALL_SCALE = 0.05

        def _routing(x2d, gate_w):
            logits = x2d @ gate_w.T
            rw = jax.nn.softmax(logits.astype(jnp.float32), axis=-1)
            scores = jax.nn.sigmoid(logits.astype(jnp.float32))
            _, sel = jax.lax.top_k(scores, TOP_K)
            w = jnp.take_along_axis(rw, sel, axis=-1)
            w = w / w.sum(axis=-1, keepdims=True)
            return (w.astype(x2d.dtype), sel)

        def _moe(x2d, Wg, Wu, Wd, cw):
            g = jnp.einsum('th,ehi->eti', x2d, Wg)
            u = jnp.einsum('th,ehi->eti', x2d, Wu)
            a = jax.nn.silu(g) * u * cw.T[:, :, None]
            return jnp.einsum('eti,eih->th', a, Wd)
        key = jax.random.key(seed)
        ks = jax.random.split(key, 8)
        s = 0.02
        B, S = (2, 256)
        return {'hidden_states': jax.random.normal(ks[0], (B, S, HIDDEN), jnp.float32), 'gate_w': jax.random.normal(ks[1], (NUM_EXPERTS, HIDDEN), jnp.float32) * s, 'Wg': jax.random.normal(ks[2], (NUM_EXPERTS, HIDDEN, MOE_INTER), jnp.float32) * s, 'Wu': jax.random.normal(ks[3], (NUM_EXPERTS, HIDDEN, MOE_INTER), jnp.float32) * s, 'Wd': jax.random.normal(ks[4], (NUM_EXPERTS, MOE_INTER, HIDDEN), jnp.float32) * s, 'cWg': jax.random.normal(ks[5], (NUM_CHUNK, HIDDEN, CHUNK_INTER), jnp.float32) * s, 'cWu': jax.random.normal(ks[6], (NUM_CHUNK, HIDDEN, CHUNK_INTER), jnp.float32) * s, 'cWd': jax.random.normal(ks[7], (NUM_CHUNK, CHUNK_INTER, HIDDEN), jnp.float32) * s}
    _L0_ffn_all = _L0_ffn_setup()
    _L0_ffn_in = {k: v for k, v in _L0_ffn_all.items() if k in ('gate_w', 'Wg', 'Wu', 'Wd', 'cWg', 'cWu', 'cWd')}
    del _L0_ffn_all
    return {'x': x, 'ctx_2048': ctx_2048, 'L0_attn_Wq': _L0_attn_in['Wq'], 'L0_attn_bq': _L0_attn_in['bq'], 'L0_attn_Wk': _L0_attn_in['Wk'], 'L0_attn_bk': _L0_attn_in['bk'], 'L0_attn_Wv': _L0_attn_in['Wv'], 'L0_attn_bv': _L0_attn_in['bv'], 'L0_attn_Wo': _L0_attn_in['Wo'], 'L0_attn_bo': _L0_attn_in['bo'], 'L0_xattn_ln_w': _L0_xattn_in['ln_w'], 'L0_xattn_ln_b': _L0_xattn_in['ln_b'], 'L0_xattn_wq': _L0_xattn_in['wq'], 'L0_xattn_wq_scale': _L0_xattn_in['wq_scale'], 'L0_xattn_q_in_scale': _L0_xattn_in['q_in_scale'], 'L0_xattn_wqx': _L0_xattn_in['wqx'], 'L0_xattn_wqx_scale': _L0_xattn_in['wqx_scale'], 'L0_xattn_qx_in_scale': _L0_xattn_in['qx_in_scale'], 'L0_xattn_wk': _L0_xattn_in['wk'], 'L0_xattn_wk_scale': _L0_xattn_in['wk_scale'], 'L0_xattn_k_in_scale': _L0_xattn_in['k_in_scale'], 'L0_xattn_wv': _L0_xattn_in['wv'], 'L0_xattn_wv_scale': _L0_xattn_in['wv_scale'], 'L0_xattn_v_in_scale': _L0_xattn_in['v_in_scale'], 'L0_xattn_w_kv_x': _L0_xattn_in['w_kv_x'], 'L0_xattn_qln_w': _L0_xattn_in['qln_w'], 'L0_xattn_qln_b': _L0_xattn_in['qln_b'], 'L0_xattn_kln_w': _L0_xattn_in['kln_w'], 'L0_xattn_kln_b': _L0_xattn_in['kln_b'], 'L0_xattn_qxln_w': _L0_xattn_in['qxln_w'], 'L0_xattn_qxln_b': _L0_xattn_in['qxln_b'], 'L0_xattn_kxln_w': _L0_xattn_in['kxln_w'], 'L0_xattn_kxln_b': _L0_xattn_in['kxln_b'], 'L0_xattn_wproj': _L0_xattn_in['wproj'], 'L0_xattn_proj_w_scale': _L0_xattn_in['proj_w_scale'], 'L0_xattn_proj_in_scale': _L0_xattn_in['proj_in_scale'], 'L0_xattn_proj_smooth': _L0_xattn_in['proj_smooth'], 'L0_ffn_gate_w': _L0_ffn_in['gate_w'], 'L0_ffn_Wg': _L0_ffn_in['Wg'], 'L0_ffn_Wu': _L0_ffn_in['Wu'], 'L0_ffn_Wd': _L0_ffn_in['Wd'], 'L0_ffn_cWg': _L0_ffn_in['cWg'], 'L0_ffn_cWu': _L0_ffn_in['cWu'], 'L0_ffn_cWd': _L0_ffn_in['cWd']}

def reference(x, ctx_2048, L0_attn_Wq, L0_attn_bq, L0_attn_Wk, L0_attn_bk, L0_attn_Wv, L0_attn_bv, L0_attn_Wo, L0_attn_bo, L0_xattn_ln_w, L0_xattn_ln_b, L0_xattn_wq, L0_xattn_wq_scale, L0_xattn_q_in_scale, L0_xattn_wqx, L0_xattn_wqx_scale, L0_xattn_qx_in_scale, L0_xattn_wk, L0_xattn_wk_scale, L0_xattn_k_in_scale, L0_xattn_wv, L0_xattn_wv_scale, L0_xattn_v_in_scale, L0_xattn_w_kv_x, L0_xattn_qln_w, L0_xattn_qln_b, L0_xattn_kln_w, L0_xattn_kln_b, L0_xattn_qxln_w, L0_xattn_qxln_b, L0_xattn_kxln_w, L0_xattn_kxln_b, L0_xattn_wproj, L0_xattn_proj_w_scale, L0_xattn_proj_in_scale, L0_xattn_proj_smooth, L0_ffn_gate_w, L0_ffn_Wg, L0_ffn_Wu, L0_ffn_Wd, L0_ffn_cWg, L0_ffn_cWu, L0_ffn_cWd):
    import jax
    import jax.numpy as jnp

    def _L0_attn_ref(x, Wq, bq, Wk, bk, Wv, bv, Wo, bo):
        import jax, jax.numpy as jnp
        import numpy as np
        B, T, D = (2, 256, 256)
        HQ, HKV = (32, 8)
        HD = D // HQ
        G = HQ // HKV
        ROPE_BASE = 10000.0

        def _rope(q, k):
            t, d = (q.shape[2], q.shape[3])
            inv_freq = 1.0 / ROPE_BASE ** (jnp.arange(0, d, 2, dtype=jnp.float32) / d)
            ang = jnp.arange(t, dtype=jnp.float32)[:, None] * inv_freq[None, :]
            cos = jnp.concatenate([jnp.cos(ang), jnp.cos(ang)], axis=-1)[None, None]
            sin = jnp.concatenate([jnp.sin(ang), jnp.sin(ang)], axis=-1)[None, None]

            def rot_half(x):
                x1, x2 = jnp.split(x, 2, axis=-1)
                return jnp.concatenate([-x2, x1], axis=-1)
            return (q * cos + rot_half(q) * sin, k * cos + rot_half(k) * sin)
        b, t, _ = x.shape
        Q = (x @ Wq.T + bq).reshape(b, t, HQ, HD).transpose(0, 2, 1, 3)
        K = (x @ Wk.T + bk).reshape(b, t, HKV, HD).transpose(0, 2, 1, 3)
        V = (x @ Wv.T + bv).reshape(b, t, HKV, HD).transpose(0, 2, 1, 3)
        Q, K = _rope(Q, K)
        K = jnp.repeat(K, G, axis=1)
        V = jnp.repeat(V, G, axis=1)
        scores = jnp.einsum('bhqd,bhkd->bhqk', Q, K) / np.sqrt(HD).astype(np.float32)
        w = jax.nn.softmax(scores, axis=-1)
        attn = jnp.einsum('bhqk,bhkd->bhqd', w, V)
        out = attn.transpose(0, 2, 1, 3).reshape(b, t, D)
        return out @ Wo.T + bo

    def _L0_xattn_ref(hidden_states, cond, ln_w, ln_b, wq, wq_scale, q_in_scale, wqx, wqx_scale, qx_in_scale, wk, wk_scale, k_in_scale, wv, wv_scale, v_in_scale, w_kv_x, qln_w, qln_b, kln_w, kln_b, qxln_w, qxln_b, kxln_w, kxln_b, wproj, proj_w_scale, proj_in_scale, proj_smooth):
        import jax, jax.numpy as jnp
        import numpy as np
        FP8_MAX = 448.0
        EPS = 1e-05

        def _fp8_roundtrip(x):
            return x.astype(jnp.float8_e4m3fn).astype(jnp.float32)

        def _div_clamp_fp8(x, scale):
            y = jnp.clip(x.astype(jnp.float32) / scale, -FP8_MAX, FP8_MAX)
            y = y.astype(jnp.bfloat16).astype(jnp.float32)
            return _fp8_roundtrip(y)

        def _ln(x, w, b):
            mu = jnp.mean(x, axis=-1, keepdims=True)
            var = jnp.mean(jnp.square(x - mu), axis=-1, keepdims=True)
            return (x - mu) * jax.lax.rsqrt(var + EPS) * w + b

        def _fp8_linear_pertensor(x, wq, w_scale, in_scale):
            xq = _div_clamp_fp8(x, in_scale)
            return jnp.einsum('bsi,oi->bso', xq * in_scale, wq) * w_scale

        def _gqa(q, k, v):
            scale = 1.0 / np.sqrt(q.shape[-1])
            scores = jnp.einsum('bsghd,btgd->bghst', q, k) * scale
            p = jax.nn.softmax(scores, axis=-1)
            return jnp.einsum('bghst,btgd->bsghd', p, v)
        b, s, _ = hidden_states.shape
        sc = cond.shape[1]
        d = qln_w.shape[0]
        nh = wq.shape[0] // d
        g = wk.shape[0] // d
        hpg = nh // g
        ln_out = _ln(hidden_states, ln_w, ln_b)
        q = _fp8_linear_pertensor(ln_out, wq, wq_scale, q_in_scale).reshape(b, s, g, hpg, d)
        q = _ln(q, qln_w, qln_b)
        k = _fp8_linear_pertensor(ln_out, wk, wk_scale, k_in_scale).reshape(b, s, g, d)
        k = _ln(k, kln_w, kln_b)
        v = _fp8_linear_pertensor(ln_out, wv, wv_scale, v_in_scale).reshape(b, s, g, d)
        core = _gqa(q, k, v).reshape(b, s, nh * d)
        qx = _fp8_linear_pertensor(ln_out, wqx, wqx_scale, qx_in_scale).reshape(b, s, g, hpg, d)
        qx = _ln(qx, qxln_w, qxln_b)
        kvx = jnp.einsum('bsi,oi->bso', cond, w_kv_x)
        kx, vx = jnp.split(kvx, 2, axis=-1)
        kx = _ln(kx.reshape(b, sc, g, d), kxln_w, kxln_b)
        vx = vx.reshape(b, sc, g, d)
        xout = _gqa(qx, kx, vx).reshape(b, s, nh * d)
        cat = jnp.concatenate([core, xout], axis=-1)
        catq = _div_clamp_fp8(cat, proj_smooth)
        return jnp.einsum('bsi,oi->bso', catq, wproj) * (proj_in_scale * proj_w_scale)

    def _L0_ffn_ref(hidden_states, gate_w, Wg, Wu, Wd, cWg, cWu, cWd):
        import jax, jax.numpy as jnp
        import numpy as np
        HIDDEN = 256
        NUM_EXPERTS = 32
        TOP_K = 4
        MOE_INTER = 96
        GROUP = 2
        NUM_CHUNK = NUM_EXPERTS // GROUP
        CHUNK_INTER = 128
        SMALL_SCALE = 0.05

        def _routing(x2d, gate_w):
            logits = x2d @ gate_w.T
            rw = jax.nn.softmax(logits.astype(jnp.float32), axis=-1)
            scores = jax.nn.sigmoid(logits.astype(jnp.float32))
            _, sel = jax.lax.top_k(scores, TOP_K)
            w = jnp.take_along_axis(rw, sel, axis=-1)
            w = w / w.sum(axis=-1, keepdims=True)
            return (w.astype(x2d.dtype), sel)

        def _moe(x2d, Wg, Wu, Wd, cw):
            g = jnp.einsum('th,ehi->eti', x2d, Wg)
            u = jnp.einsum('th,ehi->eti', x2d, Wu)
            a = jax.nn.silu(g) * u * cw.T[:, :, None]
            return jnp.einsum('eti,eih->th', a, Wd)
        B, S, H = hidden_states.shape
        T = B * S
        x = hidden_states.reshape(T, H)
        w, sel = _routing(x, gate_w)
        rows = jnp.arange(T)[:, None]
        cw_large = jnp.zeros((T, NUM_EXPERTS), x.dtype).at[rows, sel].add(w)
        cw_small = jnp.zeros((T, NUM_CHUNK), x.dtype).at[rows, sel // GROUP].add(w)
        large = _moe(x, Wg, Wu, Wd, cw_large)
        small = _moe(x, cWg, cWu, cWd, cw_small)
        return (large + SMALL_SCALE * small).reshape(B, S, H)
    x = _layernorm(x + _L0_attn_ref(x, L0_attn_Wq, L0_attn_bq, L0_attn_Wk, L0_attn_bk, L0_attn_Wv, L0_attn_bv, L0_attn_Wo, L0_attn_bo), axis=-1)
    x = _layernorm(x + _L0_xattn_ref(x, ctx_2048, L0_xattn_ln_w, L0_xattn_ln_b, L0_xattn_wq, L0_xattn_wq_scale, L0_xattn_q_in_scale, L0_xattn_wqx, L0_xattn_wqx_scale, L0_xattn_qx_in_scale, L0_xattn_wk, L0_xattn_wk_scale, L0_xattn_k_in_scale, L0_xattn_wv, L0_xattn_wv_scale, L0_xattn_v_in_scale, L0_xattn_w_kv_x, L0_xattn_qln_w, L0_xattn_qln_b, L0_xattn_kln_w, L0_xattn_kln_b, L0_xattn_qxln_w, L0_xattn_qxln_b, L0_xattn_kxln_w, L0_xattn_kxln_b, L0_xattn_wproj, L0_xattn_proj_w_scale, L0_xattn_proj_in_scale, L0_xattn_proj_smooth), axis=-1)
    x = _layernorm(x + _L0_ffn_ref(x, L0_ffn_gate_w, L0_ffn_Wg, L0_ffn_Wu, L0_ffn_Wd, L0_ffn_cWg, L0_ffn_cWu, L0_ffn_cWd), axis=-1)
    return x

_drawn_inputs = setup_inputs


def setup_inputs(seed=0):
    import zlib

    import numpy as np

    out = dict(_drawn_inputs(seed))
    spreads = {'L0_attn_bq': (0.0, 0.8),
     'L0_attn_bk': (0.0, 0.8),
     'L0_attn_bv': (0.0, 0.1),
     'L0_attn_bo': (0.0, 0.1),
     'L0_xattn_ln_w': (1.0, 0.6),
     'L0_xattn_ln_b': (0.0, 0.1),
     'L0_xattn_q_in_scale': (0.05000000074505806, 0.6),
     'L0_xattn_qx_in_scale': (0.05000000074505806, 0.6),
     'L0_xattn_k_in_scale': (0.05000000074505806, 0.6),
     'L0_xattn_v_in_scale': (0.05000000074505806, 0.6),
     'L0_xattn_qln_w': (1.0, 0.6),
     'L0_xattn_qln_b': (0.0, 0.8),
     'L0_xattn_kln_w': (1.0, 0.6),
     'L0_xattn_kln_b': (0.0, 0.8),
     'L0_xattn_qxln_w': (1.0, 0.6),
     'L0_xattn_qxln_b': (0.0, 0.8),
     'L0_xattn_kxln_w': (1.0, 0.6),
     'L0_xattn_kxln_b': (0.0, 0.8),
     'L0_xattn_proj_smooth': (0.05000000074505806, 0.2)}
    factors = {'L0_attn_Wq': 8.0,
     'L0_attn_Wk': 8.0,
     'L0_attn_Wv': 5.682,
     'L0_ffn_gate_w': 8.0,
     'L0_ffn_Wg': 8.0,
     'L0_ffn_Wu': 8.0,
     'L0_ffn_Wd': 8.0,
     'L0_ffn_cWg': 8.0,
     'L0_ffn_cWu': 8.0,
     'L0_ffn_cWd': 8.0}
    for name, (base, spread) in spreads.items():
        noise = np.random.default_rng([zlib.crc32(name.encode()), seed]).standard_normal(out[name].shape)
        drawn = base * np.exp(spread * noise) if base else spread * noise
        out[name] = jnp.asarray(drawn.astype(out[name].dtype))
    for name, factor in factors.items():
        out[name] = (out[name] * factor).astype(out[name].dtype)
    return out
```

```python
from contextlib import ExitStack

import concourse.bass as bass
from concourse import mybir

ALU = mybir.AluOpType
ACT = mybir.ActivationFunctionType
F32 = mybir.dt.float32
F32R = mybir.dt.float32r
BF16 = mybir.dt.bfloat16
U16 = mybir.dt.uint16
I32 = mybir.dt.int32
AX_X = mybir.AxisListType.X

P = 128
NB = 16
T = 128
NT = NB * T
D = 256
KC = D // P
EPS = 1e-5

HKV, G, HD = 8, 4, 8
QKV = D + 2 * HKV * HD
TERMS = 3
HALF = HKV // 2
STACK = TERMS * HALF * HD
PVW = HKV * HD + HKV
A_GROUPS = 2 * G


def ap_bcast(ap, axis, n):
    a = ap.unsqueeze(axis)
    shape = list(a.shape)
    shape[axis] = n
    return a.to_broadcast(shape)


def rsqrt_steps(dve, link, var, half, bits, tmp, y):
    link(dve.tensor_scalar(half, var, -0.5, None, ALU.mult))
    link(dve.tensor_scalar(bits, var.bitcast(I32), 1, None, ALU.logical_shift_right))
    link(dve.tensor_scalar(y.bitcast(I32), bits, -1.0, float(0x5F3759DF), ALU.mult, ALU.add))
    for _ in range(3):
        link(dve.tensor_tensor(tmp, y, y, ALU.mult))
        link(dve.tensor_tensor(tmp, tmp, half, ALU.mult))
        link(dve.scalar_tensor_tensor(out=y, in0=tmp, scalar=1.5, in1=y, op0=ALU.add, op1=ALU.mult))


RSQRT_LINKS = 12


def mean_var_steps(dve, link, stats, mean, var, tmp):
    m0, m1 = stats[:, :, 1], stats[:, :, 4]
    link(dve.tensor_tensor(mean, m0, m1, ALU.add))
    link(dve.tensor_scalar(mean, mean, 0.5, None, ALU.mult))
    link(dve.tensor_tensor(tmp, m0, m1, ALU.subtract))
    link(dve.scalar_tensor_tensor(out=tmp, in0=tmp, scalar=0.25, in1=tmp, op0=ALU.mult, op1=ALU.mult))
    link(dve.tensor_tensor(var, stats[:, :, 2], stats[:, :, 5], ALU.add))
    link(dve.scalar_tensor_tensor(out=var, in0=var, scalar=1.0 / D, in1=tmp, op0=ALU.mult, op1=ALU.add))
    link(dve.tensor_scalar(var, var, EPS, None, ALU.add))


class Chain:

    def __init__(self, eng, sem):
        self.eng, self.sem, self.base, self.n, self.done, self.loops = eng, sem, 0, 0, 0, []

    def link(self, ins):
        ins.then_inc(self.sem, 1)
        self.n += 1
        self.done += 1
        self.eng.wait_ge(self.sem, self.base + self.n)

    def enter(self, i, per):
        start = self.base + self.n
        self.loops.append((start, per, self.done))
        self.base, self.n, self.done = start + i * per, 0, 0

    def leave(self, rounds):
        start, per, done = self.loops.pop()
        assert self.done == per, (self.done, per)
        self.base, self.n, self.done = start + rounds * per, 0, done + rounds * per


def program(nc, a):
    with ExitStack() as ctx:
        build(nc, a, ctx)


def build(nc, a, ctx):
    def sb(name, shape, dt):
        return ctx.enter_context(nc.sbuf_tensor("sb_" + name, shape, dt))

    def sem(name):
        return ctx.enter_context(nc.semaphore(name))

    banks = [ctx.enter_context(nc.psum_tensor(f"bank{i}", [P, 512], F32)) for i in range(8)]

    xres = sb("xres", [P, NB, D], F32)
    stats = sb("stats", [P, NB, 6], F32)
    mean, var, half, tmp, rstd = (sb(n, [P, NB], F32) for n in ("mean", "var", "half", "tmp", "rstd"))
    bits = sb("bits", [P, NB], I32)
    ident = sb("ident", [P, P], F32)

    small = dict(stats=stats, mean=mean, var=var, half=half, tmp=tmp, rstd=rstd, bits=bits)

    stage_a(nc, a, sem, banks, xres, stats, ident)
    with ExitStack() as mid:
        xq = mid.enter_context(nc.sbuf_tensor("sb_xq", [P, 4, KC, NT], BF16))
        stage_l(nc, a, sem, banks, xres, small, ident, xq)
        stage_b(nc, a, sem, banks, xres, ident, xq)
    stage_c(nc, a, sem, banks, xres, small, ident)


def stage_a(nc, a, sem, banks, xres, stats, ident):
    inner = ExitStack()

    def sb(name, shape, dt):
        return inner.enter_context(nc.sbuf_tensor("sb_" + name, shape, dt))

    bank_qkv, bank_stack, bank_s0, bank_s1, bank_p0, bank_p1, bank_o, bank_y = banks
    bank_s, bank_p = (bank_s0, bank_s1), (bank_p0, bank_p1)

    xT = sb("xT", [P, KC, NT], F32)
    w_qkv = sb("w_qkv", [P, KC, QKV], F32)
    w_qkv_h, w_qkv_l = sb("w_qkv_h", [P, KC, QKV], F32R), sb("w_qkv_l", [P, KC, QKV], F32R)
    w_o = sb("w_o", [P, KC, D], F32)
    w_o_h, w_o_l = sb("w_o_h", [P, KC, D], F32R), sb("w_o_l", [P, KC, D], F32R)
    b_qkv, b_o = sb("b_qkv", [P, QKV], F32), sb("b_o", [P, D], F32)
    rope = sb("rope", [P, 2, HD], F32)
    gmask = sb("gmask", [STACK, HALF], F32)
    xh = [sb(f"xh{i}", [P, KC, P], F32R) for i in range(2)]
    xl = [sb(f"xl{i}", [P, KC, P], F32R) for i in range(2)]
    qkv = sb("qkv", [P, QKV], F32)
    rot = sb("rot", [P, QKV - HKV * HD], F32)
    q_stack = sb("q_stack", [P, 2 * G, TERMS, HALF * HD], F32R)
    k_stack = sb("k_stack", [P, 2, TERMS, HALF * HD], F32R)
    qT = [sb(f"qT{i}", [STACK, 2 * G, P], F32R) for i in range(2)]
    kbd = [sb(f"kbd{i}", [STACK, 2, HALF, P], F32R) for i in range(2)]
    v_h = [sb(f"v_h{i}", [P, (HKV + 1) * PVW], F32R) for i in range(2)]
    v_l = [sb(f"v_l{i}", [P, (HKV + 1) * PVW], F32R) for i in range(2)]
    smax = [sb(f"smax{i}", [P, HALF], F32) for i in range(2)]
    probs = [sb(f"probs{i}", [P, HALF, P], F32) for i in range(2)]
    pT_h = [sb(f"pT_h{i}", [P, HALF, G, P], F32R) for i in range(2)]
    pT_l = [sb(f"pT_l{i}", [P, HALF, G, P], F32R) for i in range(2)]
    oT = sb("oT", [PVW, G, P], F32)
    rsum = sb("rsum", [P, G, HKV], F32)
    attn = sb("attn", [P, HKV, G, HD], F32)
    aT_h, aT_l = sb("aT_h", [P, KC, P], F32R), sb("aT_l", [P, KC, P], F32R)
    y = sb("y_a", [P, D], F32)

    loaded = sem("a_loaded")
    w_high, w_low = sem("a_w_high"), sem("a_w_low")
    zeroed = sem("a_zeroed")
    x_h, x_l = sem("a_x_h"), sem("a_x_l")
    qkv_ready, qkv_used = sem("qkv_ready"), sem("qkv_used")
    stacked = sem("stacked")
    stackT_ready, stackT_used = sem("stackT_ready"), sem("stackT_used")
    v_ready, k_ready = sem("v_ready"), sem("k_ready")
    s_ready, s_used = sem("s_ready"), sem("s_used")
    shifted, p_ready = sem("shifted"), sem("p_ready")
    pT_ready, pT_high, pT_low = sem("pT_ready"), sem("pT_high"), sem("pT_low")
    pv_half = sem("pv_half")
    oT_kept = sem("oT_kept")
    o_ready, attn_ready = sem("o_ready"), sem("attn_ready")
    aT_ready, aT_high, aT_low = sem("aT_ready"), sem("aT_high"), sem("aT_low")
    y_ready, y_used = sem("y_ready"), sem("y_used")
    a_dve = sem("a_dve")

    NLOAD = 9

    def run(eng, front, back, first, ctx_chain=None, per=0):
        first()
        back(0, 0, False, True)
        with eng.Fori(0, (NB - 2) // 2) as i:
            if ctx_chain:
                ctx_chain.enter(i, per)
            for k in (1, 2):
                back(2 * i + k, k % 2, True, True)
            if ctx_chain:
                ctx_chain.leave((NB - 2) // 2)
        back(NB - 1, 1, True, False)

    with inner, nc.Block() as block:

        @block.sync
        def _(sp):
            sp.dma_start(xT[:], a["xT"].rearrange("(c p) t -> p c t", p=P)).then_inc(loaded, 16)
            sp.dma_start(w_qkv[:], a["w_qkvT"].rearrange("(c p) n -> p c n", p=P)).then_inc(loaded, 16)
            sp.dma_start(b_qkv[:], a["b_qkv"].to_broadcast([P, QKV])).then_inc(loaded, 16)
            sp.dma_start(rope[:], a["rope"]).then_inc(loaded, 16)
            sp.dma_start(ident[:], a["ident"]).then_inc(loaded, 16)
            sp.dma_start(gmask[:], a["gmask"]).then_inc(loaded, 16)
            sp.dma_start(w_o[:], a["w_oT"].rearrange("(c p) n -> p c n", p=P)).then_inc(loaded, 16)
            sp.dma_start(b_o[:], a["b_o"].to_broadcast([P, D])).then_inc(loaded, 16)
            sp.dma_start(xres[:], a["x"].rearrange("b t d -> t b d")).then_inc(loaded, 16)

        @block.scalar
        def _(act):
            act.wait_ge(loaded, 16 * NLOAD)
            act.activation(w_qkv_h[:], w_qkv[:], ACT.Copy).then_inc(w_high, 1)
            act.activation(w_o_h[:], w_o[:], ACT.Copy).then_inc(w_high, 1)

            def split_x(b, par):
                if not (isinstance(b, int) and b < 2):
                    act.wait_ge(qkv_ready, b - 1)
                act.wait_ge(loaded, 16 * NLOAD)
                act.activation(xh[par][:], xT[:, :, bass.ds(b * P, P)], ACT.Copy).then_inc(x_h, 1)

            def keep_qT(b, par, r):
                act.wait_ge(stackT_ready, 3 * b + r + 1)
                if not (isinstance(b, int) and b < 2):
                    act.wait_ge(s_ready, 8 * (b - 1))
                act.activation(qT[par][:, r * G:(r + 1) * G, :],
                               bank_stack[0:STACK, :].rearrange("p (j t) -> p j t", j=G),
                               ACT.Copy).then_inc(stackT_used, 1)

            def exps(b, n):
                act.wait_ge(shifted, 8 * b + n + 1)
                act.activation(probs[n % 2][:], probs[n % 2][:], ACT.Exp, scale=float(HD) ** -0.5).then_inc(p_ready, 1)

            def high(b, n):
                h = n // G
                act.wait_ge(pT_ready, 8 * b + n + 1)
                if not (isinstance(b, int) and b == 0):
                    act.wait_ge(pv_half, 2 * b + h - 1)
                act.activation(pT_h[h][:, :, n % G, :], bank_p[n % 2][:].rearrange("p (g t) -> p g t", g=HALF),
                               ACT.Copy).then_inc(pT_high, 1)

            def first():
                split_x(0, 0)
                keep_qT(0, 0, 0)
                keep_qT(0, 0, 1)
                exps(0, 0)

            def back(b, par, tail, front):
                for n in range(8):
                    high(b, n)
                    if n == 0 and tail:
                        act.wait_ge(pv_half, 2 * b)
                        act.activation(oT[:].rearrange("p j t -> p (j t)"), bank_o[0:PVW, :], ACT.Copy).then_inc(oT_kept, 1)
                    if n == 1 and front:
                        split_x(b + 1, 1 - par)
                    if n == 3 and tail:
                        keep_aT(b - 1)
                    if n == 5 and front:
                        keep_qT(b + 1, 1 - par, 0)
                    if n == 6 and front:
                        keep_qT(b + 1, 1 - par, 1)
                    if n < 7:
                        exps(b, n + 1)
                    elif front:
                        exps(b + 1, 0)

            def keep_aT(b):
                act.wait_ge(aT_ready, b + 1)
                act.activation(aT_h[:], bank_y[:, 0:D].rearrange("p (c t) -> p c t", c=KC), ACT.Copy).then_inc(aT_high, 1)

            run(act, None, back, first)
            act.wait_ge(pv_half, 2 * NB)
            act.activation(oT[:].rearrange("p j t -> p (j t)"), bank_o[0:PVW, :], ACT.Copy).then_inc(oT_kept, 1)
            keep_aT(NB - 1)

        @block.gpsimd
        def _(pool):
            for i in range(2):
                pool.memset(v_h[i][:].bitcast(F32), 0.0).then_inc(zeroed, 1)
                pool.memset(v_l[i][:].bitcast(F32), 0.0).then_inc(zeroed, 1)
            pool.wait_ge(zeroed, 4)
            for i in range(2):
                ones = v_h[i][:, HKV * HD:HKV * HD + HKV * (PVW + 1)]
                ones = ones.rearrange("p (g c) -> p g c", g=HKV)[:, :, 0]
                pool.memset(ones.bitcast(F32), 1.0).then_inc(zeroed, 1)

        @block.vector
        def _(dve):
            chain = Chain(dve, a_dve)
            link = chain.link
            dve.sem_inc(y_used, 1)
            dve.wait_ge(loaded, 16 * NLOAD)
            dve.wait_ge(w_high, 2)
            dve.tensor_tensor(w_qkv_l[:], w_qkv[:], w_qkv_h[:].bitcast(F32), ALU.subtract).then_inc(w_low, 1)
            dve.tensor_tensor(w_o_l[:], w_o[:], w_o_h[:].bitcast(F32), ALU.subtract).then_inc(w_low, 1)
            dve.wait_ge(zeroed, 6)

            def split_x(b, par):
                dve.wait_ge(x_h, b + 1)
                dve.tensor_tensor(xl[par][:], xT[:, :, bass.ds(b * P, P)], xh[par][:].bitcast(F32),
                                  ALU.subtract).then_inc(x_l, 1)

            def rotate(b, par):
                dve.wait_ge(qkv_ready, b + 1)
                ins = dve.tensor_tensor(qkv[:], bank_qkv[:, 0:QKV], b_qkv[:], ALU.add)
                ins.then_inc(qkv_used, 1)
                dve.wait_ge(qkv_used, b + 1)
                heads = (QKV - HKV * HD) // HD
                src = qkv[:, 0:heads * HD].rearrange("p (h d) -> p h d", d=HD)
                dst = rot[:].rearrange("p (h d) -> p h d", d=HD)
                hh = HD // 2
                dve.tensor_tensor(dst[:, :, 0:hh], src[:, :, hh:HD], ap_bcast(rope[:, 1, 0:hh], 1, heads), ALU.mult)
                link(dve.tensor_tensor(dst[:, :, hh:HD], src[:, :, 0:hh], ap_bcast(rope[:, 1, hh:HD], 1, heads), ALU.mult))
                link(dve.tensor_tensor(src, src, ap_bcast(rope[:, 0, :], 1, heads), ALU.mult))
                link(dve.tensor_tensor(rot[:], rot[:], qkv[:, 0:heads * HD], ALU.add))
                q = rot[:, 0:D].rearrange("p (j c) -> p j c", j=2 * G)
                k = rot[:, D:D + HKV * HD].rearrange("p (h c) -> p h c", h=2)
                if not (isinstance(b, int) and b == 0):
                    dve.wait_ge(stackT_ready, 3 * b)
                dve.tensor_copy(q_stack[:, :, 0, :], q)
                link(dve.tensor_copy(k_stack[:, :, 0, :], k))
                dve.tensor_copy(q_stack[:, :, 1, :], q)
                dve.tensor_copy(k_stack[:, :, 2, :], k)
                dve.tensor_tensor(q_stack[:, :, 2, :], q, q_stack[:, :, 0, :].bitcast(F32), ALU.subtract)
                dve.tensor_tensor(k_stack[:, :, 1, :], k, k_stack[:, :, 0, :].bitcast(F32),
                                  ALU.subtract).then_inc(stacked, 1)
                v = qkv[:, D + HKV * HD:QKV].rearrange("p (g d) -> p g d", g=HKV)
                step = PVW + HD
                vh = v_h[par][:, 0:HKV * step].rearrange("p (g c) -> p g c", g=HKV)[:, :, 0:HD]
                vl = v_l[par][:, 0:HKV * step].rearrange("p (g c) -> p g c", g=HKV)[:, :, 0:HD]
                if not (isinstance(b, int) and b < 2):
                    dve.wait_ge(pv_half, 2 * (b - 1))
                link(dve.tensor_copy(vh, v))
                dve.tensor_tensor(vl, v, vh.bitcast(F32), ALU.subtract).then_inc(v_ready, 1)

            def spread_k(b, par):
                dve.wait_ge(stackT_ready, 3 * b + 3)
                if not (isinstance(b, int) and b < 2):
                    dve.wait_ge(s_ready, 8 * (b - 1))
                for h in range(2):
                    src = ap_bcast(bank_stack[0:STACK, h * P:(h + 1) * P], 1, HALF)
                    ins = dve.tensor_tensor(kbd[par][:, h], src, ap_bcast(gmask[:], 2, P), ALU.mult)
                ins.then_inc(stackT_used, 1)

            def shift(b, n):
                dve.wait_ge(s_ready, 8 * b + n + 1)
                s3 = bank_s[n % 2][:].rearrange("p (g k) -> p g k", g=HALF)
                if not (isinstance(b, int) and b == 0 and n < 2):
                    dve.wait_ge(pT_ready, 8 * b + n - 1)
                link(dve.tensor_reduce(smax[n % 2][:], s3, AX_X, ALU.max))
                dve.tensor_tensor(probs[n % 2][:], s3, ap_bcast(smax[n % 2][:], 2, P), ALU.subtract).then_inc(shifted, 1)

            def low(b, n):
                h = n // G
                dve.wait_ge(pT_high, 8 * b + n + 1)
                dve.tensor_tensor(pT_l[h][:, :, n % G, :], bank_p[n % 2][:].rearrange("p (g t) -> p g t", g=HALF),
                                  pT_h[h][:, :, n % G, :].bitcast(F32), ALU.subtract).then_inc(pT_low, 1)

            def normalise(b):
                dve.wait_ge(o_ready, b + 1)
                o3 = bank_y[:, 0:G * PVW].rearrange("p (j c) -> p j c", j=G)
                link(dve.reciprocal(rsum[:], o3[:, :, HKV * HD:PVW]))
                for j in range(G):
                    ins = dve.tensor_tensor(attn[:, :, j, :], o3[:, j, 0:HKV * HD].rearrange("p (g d) -> p g d", g=HKV),
                                            ap_bcast(rsum[:, j, :], 2, HD), ALU.mult)
                ins.then_inc(attn_ready, 1)

            def low_a(b):
                dve.wait_ge(aT_high, b + 1)
                dve.tensor_tensor(aT_l[:], bank_y[:, 0:D].rearrange("p (c t) -> p c t", c=KC),
                                  aT_h[:].bitcast(F32), ALU.subtract).then_inc(aT_low, 1)

            def residual(b):
                dve.wait_ge(y_ready, b + 1)
                dve.tensor_tensor(y[:], bank_y[:, 0:D], b_o[:], ALU.add).then_inc(y_used, 1)
                dve.wait_ge(y_used, b + 2)
                r = xres[:, bass.ds(b, 1), :]
                link(dve.tensor_tensor(r, r, y[:].unsqueeze(1), ALU.add))
                link(dve.bn_stats(stats[:, bass.ds(b, 1), :].rearrange("p b s -> p (b s)"), r.rearrange("p b d -> p (b d)")))

            def first():
                split_x(0, 0)
                rotate(0, 0)
                spread_k(0, 0)
                shift(0, 0)

            def back(b, par, tail, front):
                for n in range(8):
                    if n < 7:
                        shift(b, n + 1)
                    elif front:
                        shift(b + 1, 0)
                    low(b, n)
                    if n == 1:
                        if front:
                            split_x(b + 1, 1 - par)
                        if tail:
                            normalise(b - 1)
                    if n == 3 and tail:
                        low_a(b - 1)
                    if n == 3 and front:
                        rotate(b + 1, 1 - par)
                    if n == 5 and tail:
                        residual(b - 1)
                    if n == 6 and front:
                        spread_k(b + 1, 1 - par)

            run(dve, None, back, first, chain, 2 * (8 + 5 + 1 + 2))
            normalise(NB - 1)
            low_a(NB - 1)
            residual(NB - 1)

        @block.tensor
        def _(pe):
            pe.wait_ge(w_low, 2)
            pe.wait_ge(zeroed, 6)
            pe.wait_ge(loaded, 16 * NLOAD)

            def project(b, par):
                pe.wait_ge(x_h, b + 1)
                pe.wait_ge(x_l, b + 1)
                if not (isinstance(b, int) and b == 0):
                    pe.wait_ge(qkv_used, b)
                for c in range(KC):
                    pe.matmul(bank_qkv[:, 0:QKV], xh[par][:, c, :], w_qkv_h[:, c, :], start=(c == 0), stop=False)
                    pe.matmul(bank_qkv[:, 0:QKV], xh[par][:, c, :], w_qkv_l[:, c, :], start=False, stop=False)
                    mm = pe.matmul(bank_qkv[:, 0:QKV], xl[par][:, c, :], w_qkv_h[:, c, :], start=False, stop=(c == KC - 1))
                mm.then_inc(qkv_ready, 1)

            def turn_stack(b, r):
                if r == 0:
                    pe.wait_ge(stacked, b + 1)
                if not (isinstance(b, int) and b == 0 and r == 0):
                    pe.wait_ge(stackT_used, 3 * b + r)
                for j in range(G if r < 2 else 2):
                    src = q_stack[:, r * G + j] if r < 2 else k_stack[:, j]
                    mm = pe.transpose(bank_stack[0:STACK, j * P:(j + 1) * P],
                                      src.rearrange("p a c -> p (a c)").bitcast(F32), ident[:])
                mm.then_inc(stackT_ready, 1)

            def scores(b, par, n):
                if n == 0:
                    pe.wait_ge(stackT_used, 3 * b + 3)
                if not (isinstance(b, int) and b == 0 and n < 2):
                    pe.wait_ge(shifted, 8 * b + n - 1)
                h, j = n // G, n % G
                pe.matmul(bank_s[n % 2][:], qT[par][:, h * G + j, :],
                          kbd[par][:, h].rearrange("p g k -> p (g k)"), start=True, stop=True).then_inc(s_ready, 1)

            def turn_p(b, n):
                pe.wait_ge(p_ready, 8 * b + n + 1)
                if not (isinstance(b, int) and b == 0 and n < 2):
                    pe.wait_ge(pT_low, 8 * b + n - 1)
                for g in range(HALF):
                    mm = pe.transpose(bank_p[n % 2][:, g * P:(g + 1) * P], probs[n % 2][:, g, :], ident[:])
                mm.then_inc(pT_ready, 1)

            def weigh(b, par, h):
                pe.wait_ge(pT_low, 8 * b + G * (h + 1))
                if h == 0:
                    pe.wait_ge(v_ready, b + 1)
                    if not (isinstance(b, int) and b == 0):
                        pe.wait_ge(oT_kept, b)
                for g in range(HALF):
                    kv = h * HALF + g
                    ph = pT_h[h][:, g].rearrange("p j t -> p (j t)")
                    pl = pT_l[h][:, g].rearrange("p j t -> p (j t)")
                    wh, wl = (v[par][:, kv * PVW:(kv + 1) * PVW] for v in (v_h, v_l))
                    pe.matmul(bank_o[0:PVW, :], wh, ph, start=(kv == 0), stop=False)
                    pe.matmul(bank_o[0:PVW, :], wh, pl, start=False, stop=False)
                    mm = pe.matmul(bank_o[0:PVW, :], wl, ph, start=False, stop=(kv == HKV - 1))
                mm.then_inc(pv_half, 1)

            def turn_o(b):
                pe.wait_ge(oT_kept, b + 1)
                pe.wait_ge(y_used, b + 1)
                for j in range(G):
                    mm = pe.transpose(bank_y[:, j * PVW:(j + 1) * PVW], oT[:, j, :], ident[0:PVW, 0:PVW])
                mm.then_inc(o_ready, 1)

            def turn_attn(b):
                pe.wait_ge(attn_ready, b + 1)
                flat = attn[:].rearrange("p g j d -> p (g j d)")
                for c in range(KC):
                    mm = pe.transpose(bank_y[:, c * P:(c + 1) * P], flat[:, c * P:(c + 1) * P], ident[:])
                mm.then_inc(aT_ready, 1)

            def out_product(b):
                pe.wait_ge(aT_low, b + 1)
                for c in range(KC):
                    pe.matmul(bank_y[:, 0:D], aT_h[:, c, :], w_o_h[:, c, :], start=(c == 0), stop=False)
                    pe.matmul(bank_y[:, 0:D], aT_h[:, c, :], w_o_l[:, c, :], start=False, stop=False)
                    mm = pe.matmul(bank_y[:, 0:D], aT_l[:, c, :], w_o_h[:, c, :], start=False, stop=(c == KC - 1))
                mm.then_inc(y_ready, 1)

            def first():
                project(0, 0)
                for r in range(3):
                    turn_stack(0, r)
                scores(0, 0, 0)
                scores(0, 0, 1)

            def back(b, par, tail, front):
                for n in range(8):
                    turn_p(b, n)
                    if n < 6:
                        scores(b, par, n + 2)
                    if n == 0 and tail:
                        turn_o(b - 1)
                    if n == 2:
                        if tail:
                            turn_attn(b - 1)
                        if front:
                            project(b + 1, 1 - par)
                    if n == 4:
                        if tail:
                            out_product(b - 1)
                        weigh(b, par, 0)
                    if n >= 5 and front:
                        turn_stack(b + 1, n - 5)
                if front:
                    scores(b + 1, 1 - par, 0)
                    scores(b + 1, 1 - par, 1)
                weigh(b, par, 1)

            run(pe, None, back, first)
            turn_o(NB - 1)
            turn_attn(NB - 1)
            out_product(NB - 1)



XG, XH, XD = 8, 2, 128
PAIRS = XG // 2
PH = 2 * XH
KINDS = 4
FP8_MAX = 448.0
COLS = dict(q=0, qx=PH * XD, kx=2 * PH * XD, vx=2 * PH * XD + 2 * XD, k=3 * PH * XD, v=3 * PH * XD + 2 * XD)
WCOLS = 4 * PH * XD


def steps_of_fp8(dve, link, y, magic):
    link(dve.tensor_scalar(y, y, FP8_MAX, -FP8_MAX, ALU.min, ALU.max))
    link(dve.tensor_scalar(magic.bitcast(U16), y.bitcast(U16), 0x7F80, 0x0040, ALU.bitwise_and, ALU.bitwise_or))
    link(dve.tensor_scalar(magic, magic, 1.5 * 2.0 ** -6, 2.0 ** 20, ALU.max, ALU.mult))


def stage_l(nc, a, sem, banks, xres, small, ident, xq):
    inner = ExitStack()

    def sb(name, shape, dt):
        return inner.enter_context(nc.sbuf_tensor("sb_" + name, shape, dt))

    stats, mean, var, half, tmp, rstd, bits = (small[n] for n in ("stats", "mean", "var", "half", "tmp", "rstd", "bits"))
    z = [sb(f"z{i}", [P, D], F32) for i in range(2)]
    lnT = sb("lnT", [P, KC, NT], F32)
    ln_wb = sb("ln_wb", [P, 2, KC], F32)
    in_scale, in_recip = sb("in_scale", [P, KINDS, KC], F32), sb("in_recip", [P, KINDS, KC], F32)
    y = [sb(f"yq{i}", [P, NT], BF16) for i in range(2)]
    magic = [sb(f"magic{i}", [P, NT], BF16) for i in range(2)]
    total = [sb(f"total{i}", [P, NT], F32) for i in range(2)]

    loaded = sem("l_loaded")
    z_ready, zT_ready, zT_kept = sem("z_ready"), sem("zT_ready"), sem("zT_kept")
    recip_ready, y_scaled, total_ready, y_rounded = (sem(n) for n in ("recip_ready", "y_scaled", "total_ready", "y_rounded"))
    magic_ready = sem("magic_ready")
    l_dve = sem("l_dve")
    steps = [(kind, c) for kind in range(KINDS) for c in range(KC)]

    with inner, nc.Block() as block:

        @block.sync
        def _(sp):
            sp.dma_start(ln_wb[:], a["ln_wb"]).then_inc(loaded, 16)
            sp.dma_start(in_scale[:], a["in_scale"]).then_inc(loaded, 16)

        @block.vector
        def _(dve):
            chain = Chain(dve, l_dve)
            link = chain.link
            dve.wait_ge(loaded, 32)
            dve.reciprocal(in_recip[:], in_scale[:]).then_inc(recip_ready, 1)
            mean_var_steps(dve, link, stats, mean[:], var[:], tmp[:])
            rsqrt_steps(dve, link, var[:], half[:], bits[:], tmp[:], rstd[:])
            with dve.Fori(0, NB // 2) as i:
                chain.enter(i, 4)
                for k in range(2):
                    b = 2 * i + k
                    r = xres[:, bass.ds(b, 1), :].rearrange("p b d -> p (b d)")
                    link(dve.tensor_scalar(r, r, mean[:, bass.ds(b, 1)], rstd[:, bass.ds(b, 1)], ALU.subtract, ALU.mult))
                    link(dve.bn_stats(stats[:, bass.ds(b, 1), :].rearrange("p b s -> p (b s)"), r))
                chain.leave(NB // 2)
            mean_var_steps(dve, link, stats, mean[:], var[:], tmp[:])
            rsqrt_steps(dve, link, var[:], half[:], bits[:], tmp[:], rstd[:])
            dve.sem_inc(zT_ready, 2)
            with dve.Fori(0, NB // 2) as i:
                for k in range(2):
                    b = 2 * i + k
                    r = xres[:, bass.ds(b, 1), :].rearrange("p b d -> p (b d)")
                    dve.wait_ge(zT_ready, b + 1)
                    dve.tensor_scalar(z[k][:], r, mean[:, bass.ds(b, 1)], rstd[:, bass.ds(b, 1)],
                                      ALU.subtract, ALU.mult).then_inc(z_ready, 1)
            for n, (kind, c) in enumerate(steps):
                dve.wait_ge(y_scaled, n + 1)
                steps_of_fp8(dve, link, y[n % 2][:], magic[n % 2][:])
                if n >= 2:
                    dve.wait_ge(y_rounded, n - 1)
                dve.tensor_tensor(total[n % 2][:], y[n % 2][:], magic[n % 2][:], ALU.add).then_inc(total_ready, 1)
                dve.wait_ge(total_ready, n + 1)
                dve.tensor_tensor(xq[:, kind, c, :], total[n % 2][:], magic[n % 2][:], ALU.subtract).then_inc(y_rounded, 1)

        @block.tensor
        def _(pe):
            pe.sem_inc(zT_kept, 2)
            with pe.Fori(0, NB // 2) as i:
                for k in range(2):
                    b = 2 * i + k
                    pe.wait_ge(zT_kept, b + 1)
                    pe.wait_ge(z_ready, b + 1)
                    for c in range(KC):
                        mm = pe.transpose(banks[k][:, c * P:(c + 1) * P], z[k][:, c * P:(c + 1) * P], ident[:])
                    mm.then_inc(zT_ready, 1)

        @block.scalar
        def _(act):
            with act.Fori(0, NB // 2) as i:
                for k in range(2):
                    b = 2 * i + k
                    for c in range(KC):
                        if c == 0:
                            act.wait_ge(zT_ready, b + 3)
                        act.wait_ge(loaded, 32)
                        ins = act.activation(lnT[:, c, bass.ds(b * T, T)], banks[k][:, c * P:(c + 1) * P], ACT.Identity,
                                             bias=ln_wb[:, 1, c:c + 1], scale=ln_wb[:, 0, c:c + 1])
                    ins.then_inc(zT_kept, 1)
            act.wait_ge(zT_kept, NB + 2)
            act.wait_ge(recip_ready, 1)
            for n, (kind, c) in enumerate(steps):
                if n >= 2:
                    act.wait_ge(y_rounded, n - 1)
                act.activation(y[n % 2][:], lnT[:, c, :], ACT.Identity, scale=in_recip[:, kind, c:c + 1]).then_inc(y_scaled, 1)


def stage_b(nc, a, sem, banks, xres, ident, xq):
    inner = ExitStack()

    def sb(name, shape, dt):
        return inner.enter_context(nc.sbuf_tensor("sb_" + name, shape, dt))

    def pair(name, shape, dt):
        return [sb(f"{name}{i}", shape, dt) for i in range(2)]

    bank_f, bank_x, bank_p, bank_s, bank_o, bank_y = banks[0:2], banks[2], banks[3], banks[4:6], banks[6], banks[7]

    ctxT = sb("ctxT", [P, KC, NT], F32)
    acc = sb("acc", [P, NB, D], F32)
    w_raw = sb("w_raw", [P, KC, WCOLS], F32)
    w_h, w_l = sb("w_h", [P, KC, WCOLS], F32R), sb("w_l", [P, KC, WCOLS], F32R)
    wmean = sb("wmean", [P, KC, 3 * PH], F32)
    wp_raw, wp = sb("wp_raw", [P, 2 * PH, D], F32), sb("wp", [P, 2 * PH, D], BF16)
    in_scale, w_scale = sb("b_in_scale", [P, KINDS, KC], F32), sb("w_scale", [P, KINDS], F32)
    fold = sb("fold", [P, KINDS, KC], F32)
    smooth, smooth_r = sb("smooth", [P, 2, XG * XH], F32), sb("smooth_r", [P, 2, XG * XH], F32)
    norm_w, norm_b = sb("norm_w", [P, 4], F32), sb("norm_b", [P, 4], F32)
    out_scale = sb("out_scale", [P, 2], F32)
    xs = pair("xs", [P, KINDS, KC, P], F32R)
    c_h, c_l = pair("c_h", [P, KC, P], F32R), pair("c_l", [P, KC, P], F32R)
    square = sb("square", [P, 3 * PH, XD], BF16)
    sumsq = sb("sumsq", [P, 3 * PH], F32)
    nvar, nhalf, ntmp, nrstd = (sb(n, [P, 3 * PH], F32) for n in ("nvar", "nhalf", "ntmp", "nrstd"))
    nbits = sb("nbits", [P, 3 * PH], I32)
    normed = sb("normed", [P, 3, PH, XD], F32)
    qT, qxT, kT = pair("qTb", [P, PH, P], F32), pair("qxT", [P, PH, P], F32), pair("kTb", [P, PH, P], F32)
    vv = pair("vv", [P, PH, XD], F32)
    negmax, bmax = sb("negmax", [P, 2, PH], F32), sb("bmax", [P, 2, PH], F32)
    psum_, precip = sb("psum_", [P, 2, PH], F32), sb("precip", [P, 2, PH], F32)
    probs = sb("b_probs", [P, 2, PH, P], F32)
    pT = sb("b_pT", [P, 2, PH, P], F32)
    yb, magic = sb("yb", [P, 2, PH, P], BF16), sb("magic_b", [P, 2, PH, P], BF16)
    total = sb("total_b", [P, 2, PH, P], F32)
    catq = sb("catq", [P, 2, PH, P], BF16)

    loaded, ctx_loaded = sem("b_loaded"), sem("ctx_loaded")
    w_loaded = sem("w_loaded")
    w_centred, w_high, w_ready = sem("w_centred"), sem("w_high"), sem("w_ready")
    pool_turn, c_split, xs_ready, f_ready = sem("pool_turn"), sem("c_split"), sem("xs_ready"), sem("f_ready")
    ss_ready, normed_ready = sem("ss_ready"), sem("normed_ready")
    x_ready, x_kept = sem("xT_ready"), sem("xT_kept")
    s_ready, max_ready, exp_done = sem("bs_ready"), sem("max_ready"), sem("exp_done")
    p_ready, pT_ready, pT_kept = sem("bp_ready"), sem("bpT_ready"), sem("bpT_kept")
    o_ready, o_used = sem("bo_ready"), sem("bo_used")
    cat_ready = sem("cat_ready")
    y_ready, y_used = sem("by_ready"), sem("by_used")
    b_dve = sem("b_dve")
    PROJ = [("q", None, 0), ("qx", None, 1), ("kx", "vx", None), ("k", "v", 2)]
    SCALE = float(XD) ** -0.5

    def units(eng, before, first, step, end, chain=None, per_pair=0, per_round=0):
        with eng.Fori(0, PAIRS) as gp:
            if chain:
                chain.enter(gp, per_pair)
            U0 = gp * NB
            before(gp)
            first(U0)
            step(U0, gp, 0, False, True)
            with eng.Fori(0, (NB - 2) // 2) as i:
                if chain:
                    chain.enter(i, per_round)
                for k in (1, 2):
                    step(U0 + 2 * i + k, gp, 2 * i + k, True, True, k % 2)
                if chain:
                    chain.leave((NB - 2) // 2)
            step(U0 + NB - 1, gp, NB - 1, True, False, 1)
            end(U0 + NB - 1, NB - 1)
            if chain:
                chain.leave(PAIRS)

    with inner, nc.Block() as block:

        @block.sync
        def _(sp):
            for dst, src in (
                (in_scale[:], a["in_scale"]),
                (w_scale[:], a["w_scale"].to_broadcast([P, KINDS])),
                (smooth[:], a["smooth"]),
                (norm_w[:], a["norm_w"]),
                (norm_b[:], a["norm_b"]),
                (out_scale[:], a["out_scale"].to_broadcast([P, 2])),
            ):
                sp.dma_start(dst, src).then_inc(loaded, 16)
            sp.dma_start(ctxT[:], a["ctxT"].rearrange("(c p) t -> p c t", p=P)).then_inc(ctx_loaded, 16)
            sp.sem_inc(w_ready, 1)
            with sp.Fori(0, PAIRS) as gp:
                sp.wait_ge(w_ready, 2 * gp + 1)
                sp.dma_start(w_raw[:], a["w_pairs"][bass.ds(gp, 1)].rearrange("a (c p) n -> p (a c) n", p=P)).then_inc(w_loaded, 16)
                sp.dma_start(wp_raw[:], a["wproj_pairs"][bass.ds(gp, 1)].rearrange("a k p n -> p (a k) n")).then_inc(w_loaded, 16)

        @block.gpsimd
        def _(pool):
            def convert(V, b, par, wait=True):
                if wait:
                    pool.wait_ge(f_ready, 4 * V - 4)
                    pool.sem_inc(pool_turn, 1)
                pool.tensor_copy(c_h[par][:], ctxT[:, :, bass.ds(b * T, T)]).then_inc(c_split, 1)
                pool.tensor_copy(xs[par][:].rearrange("p k c t -> p (k c) t"),
                                 xq[:, :, :, bass.ds(b * T, T)].rearrange("p k c t -> p (k c) t"))
                pool.wait_ge(c_split, V + 1)
                pool.sem_inc(pool_turn, 1)
                pool.tensor_tensor(c_l[par][:], ctxT[:, :, bass.ds(b * T, T)], c_h[par][:].bitcast(F32),
                                   ALU.subtract).then_inc(xs_ready, 1)

            pool.wait_ge(ctx_loaded, 16)
            convert(0, 0, 0, False)
            convert(1, 1, 1, False)
            with pool.Fori(0, PAIRS) as gp:
                with pool.Fori(1, NB // 2) as i:
                    for par in range(2):
                        convert(gp * NB + 2 * i + par, 2 * i + par, par)
                for par in range(2):
                    convert(gp * NB + NB + par, par, par)

        @block.scalar
        def _(act):
            act.wait_ge(loaded, 16 * 6)
            act.sem_inc(x_kept, 1)
            act.sem_inc(pT_kept, 1)
            act.sem_inc(exp_done, 2)

            def before(gp):
                act.wait_ge(w_centred, 2 * gp + 1)
                act.activation(w_h[:, 0], w_raw[:, 0], ACT.Copy).then_inc(w_high, 1)
                act.wait_ge(w_centred, 2 * gp + 2)
                act.activation(w_h[:, 1], w_raw[:, 1], ACT.Copy).then_inc(w_high, 1)
                act.activation(wp[:], wp_raw[:], ACT.Copy).then_inc(w_ready, 1)

            def squares(U, par, r):
                act.wait_ge(f_ready, 4 * U + r + 1)
                col = (0, PH, 2 * PH, 2 * PH + 2)[r]
                for h in range(PH if r < 2 else 2):
                    ins = act.activation(square[:, col + h, :], bank_f[r % 2][:, h * XD:(h + 1) * XD], ACT.Square,
                                         accum_out=sumsq[:, col + h:col + h + 1])
                if r >= 2:
                    ins = act.activation(vv[par][:, 2 * (r - 2):2 * (r - 2) + 2, :].rearrange("p g d -> p (g d)"),
                                         bank_f[r % 2][:, 2 * XD:4 * XD], ACT.Copy)
                if r % 2 == 1:
                    ins.then_inc(ss_ready, 1)

            def keep(U, par, r):
                act.wait_ge(x_ready, 3 * U + r + 1)
                if r < 2:
                    dst = (qT, qxT)[r][par]
                    ins = act.activation(dst[:].rearrange("p h t -> p (h t)"), bank_x[:], ACT.Identity,
                                         bias=norm_b[:, r:r + 1], scale=norm_w[:, r:r + 1])
                else:
                    for k in range(2):
                        ins = act.activation(kT[par][:, 2 * k:2 * k + 2, :].rearrange("p h t -> p (h t)"),
                                             bank_x[:, 2 * k * P:2 * (k + 1) * P], ACT.Identity,
                                             bias=norm_b[:, 2 + k:3 + k], scale=norm_w[:, 2 + k:3 + k])
                ins.then_inc(x_kept, 1)

            def exps(U, s):
                act.wait_ge(max_ready, 2 * U + s + 1)
                for h in range(PH):
                    ins = act.activation(probs[:, s, h, :], bank_s[s][:, h * P:(h + 1) * P], ACT.Exp,
                                         bias=negmax[:, s, h:h + 1], scale=SCALE, accum_out=psum_[:, s, h:h + 1])
                ins.then_inc(exp_done, 1)

            def keep_p(U, s):
                act.wait_ge(pT_ready, 2 * U + s + 1)
                act.activation(pT[:, s].rearrange("p h t -> p (h t)"), bank_p[:], ACT.Copy).then_inc(pT_kept, 1)

            def first(U0):
                for r in range(4):
                    squares(U0, 0, r)
                for r in range(3):
                    keep(U0, 0, r)

            def step(U, gp, b, tail, front, par=0):
                nxt = 1 - par
                if front:
                    squares(U + 1, nxt, 0)
                    squares(U + 1, nxt, 1)
                exps(U, 0)
                exps(U, 1)
                if front:
                    squares(U + 1, nxt, 2)
                    squares(U + 1, nxt, 3)
                keep_p(U, 0)
                keep_p(U, 1)
                if front:
                    for r in range(3):
                        keep(U + 1, nxt, r)

            units(act, before, first, step, lambda U, b: None)

        @block.vector
        def _(dve):
            chain = Chain(dve, b_dve)
            link = chain.link
            dve.wait_ge(loaded, 16 * 6)
            link(dve.memset(acc[:], 0.0))
            link(dve.reciprocal(smooth_r[:], smooth[:]))
            link(dve.tensor_tensor(fold[:], in_scale[:], ap_bcast(w_scale[:], 2, KC), ALU.mult))
            link(dve.tensor_tensor(out_scale[:, 0:1], out_scale[:, 0:1], out_scale[:, 1:2], ALU.mult))
            dve.sem_inc(normed_ready, 2)
            dve.sem_inc(o_used, 1)
            dve.sem_inc(y_used, 1)

            def before(gp):
                dve.wait_ge(w_loaded, 32 * gp + 32)
                for c in range(KC):
                    for n, name in enumerate(("q", "qx", "k", "v")):
                        wide = PH * XD if n < 2 else 2 * XD
                        w = w_raw[:, c, COLS[name]:COLS[name] + wide]
                        ins = dve.tensor_scalar(w, w, fold[:, n, c:c + 1], None, ALU.mult)
                    link(ins)
                    qs = w_raw[:, c, 0:2 * PH * XD].rearrange("p (h d) -> p h d", d=XD)
                    ks = w_raw[:, c, 2 * PH * XD:WCOLS].rearrange("p (s h d) -> p s h d", s=2, d=XD)[:, :, 0:2, :]
                    mq = wmean[:, c, 0:2 * PH]
                    mk = wmean[:, c, 2 * PH:3 * PH].rearrange("p (s h) -> p s h", s=2)
                    dve.tensor_reduce(mq, qs, AX_X, ALU.add)
                    link(dve.tensor_reduce(mk, ks, AX_X, ALU.add))
                    link(dve.tensor_scalar(wmean[:, c], wmean[:, c], 1.0 / XD, None, ALU.mult))
                    dve.tensor_tensor(qs, qs, ap_bcast(mq, 2, XD), ALU.subtract)
                    for s in range(2):
                        ins = dve.tensor_tensor(ks[:, s], ks[:, s], ap_bcast(mk[:, s], 2, XD), ALU.subtract)
                    ins.then_inc(w_centred, 1)
                for c in range(KC):
                    dve.wait_ge(w_high, 2 * gp + c + 1)
                    ins = dve.tensor_tensor(w_l[:, c], w_raw[:, c], w_h[:, c].bitcast(F32), ALU.subtract)
                ins.then_inc(w_ready, 1)

            def norms(U, n):
                dve.wait_ge(ss_ready, 2 * U + n + 1)
                cols = slice(0, 2 * PH) if n == 0 else slice(2 * PH, 3 * PH)
                link(dve.tensor_scalar(nvar[:, cols], sumsq[:, cols], 1.0 / XD, EPS, ALU.mult, ALU.add))
                rsqrt_steps(dve, link, nvar[:, cols], nhalf[:, cols], nbits[:, cols], ntmp[:, cols], nrstd[:, cols])
                if n == 0:
                    for r in range(2):
                        dve.tensor_tensor(normed[:, r], bank_f[r][:].rearrange("p (h d) -> p h d", h=PH),
                                          ap_bcast(nrstd[:, r * PH:(r + 1) * PH], 2, XD), ALU.mult).then_inc(normed_ready, 1)
                else:
                    for r in range(2):
                        dve.tensor_tensor(normed[:, 2, 2 * r:2 * r + 2], bank_f[r][:, 0:2 * XD].rearrange("p (h d) -> p h d", h=2),
                                          ap_bcast(nrstd[:, 2 * PH + 2 * r:2 * PH + 2 * r + 2], 2, XD),
                                          ALU.mult).then_inc(normed_ready, 1)

            def maxima(U, s):
                dve.wait_ge(s_ready, 2 * U + s + 1)
                link(dve.tensor_reduce(bmax[:, s], bank_s[s][:].rearrange("p (h k) -> p h k", h=PH), AX_X, ALU.max))
                dve.tensor_scalar(negmax[:, s], bmax[:, s], -SCALE, None, ALU.mult).then_inc(max_ready, 1)

            def weights(U, s):
                dve.wait_ge(exp_done, 2 * U + s + 3)
                link(dve.reciprocal(precip[:, s], psum_[:, s]))
                dve.tensor_tensor(probs[:, s], probs[:, s], ap_bcast(precip[:, s], 2, P), ALU.mult).then_inc(p_ready, 1)

            def scaled(U, s, gp):
                dve.wait_ge(o_ready, 2 * U + s + 1)
                ins = dve.tensor_tensor(yb[:, s], bank_o[:].rearrange("p (h t) -> p h t", h=PH),
                                        ap_bcast(smooth_r[:, s, bass.ds(gp * PH, PH)], 2, P), ALU.mult)
                ins.then_inc(o_used, 1)

            def round8(U):
                dve.wait_ge(o_used, 2 * U + 3)
                steps_of_fp8(dve, link, yb[:], magic[:])
                link(dve.tensor_tensor(total[:], yb[:], magic[:], ALU.add))
                dve.tensor_tensor(catq[:], total[:], magic[:], ALU.subtract).then_inc(cat_ready, 1)

            def add_out(U, b):
                dve.wait_ge(y_ready, U + 1)
                r = acc[:, bass.ds(b, 1), :]
                ins = dve.tensor_tensor(r, r, bank_y[:, 0:D].unsqueeze(1), ALU.add)
                ins.then_inc(y_used, 1)

            def first(U0):
                norms(U0, 0)
                norms(U0, 1)

            def step(U, gp, b, tail, front, par=0):
                maxima(U, 0)
                maxima(U, 1)
                if front:
                    norms(U + 1, 0)
                weights(U, 0)
                weights(U, 1)
                if tail:
                    add_out(U - 1, b - 1)
                if front:
                    norms(U + 1, 1)
                scaled(U, 0, gp)
                scaled(U, 1, gp)
                round8(U)

            norm_links = 2 * (1 + RSQRT_LINKS)
            step_links = 2 + 2 + 4
            units(dve, before, first, step, add_out, chain,
                  KC * 3 + NB * (norm_links + step_links), 2 * (norm_links + step_links))
            dve.wait_ge(y_used, PAIRS * NB + 1)
            link(dve.tensor_scalar(acc[:], acc[:], out_scale[:, 0:1], None, ALU.mult))
            link(dve.tensor_tensor(xres[:], xres[:], acc[:], ALU.add))

        @block.tensor
        def _(pe):
            def project(U, par, r):
                if r == 0:
                    pe.wait_ge(xs_ready, U + 1)
                pe.wait_ge(normed_ready, 4 * U + r + 1)
                bank = bank_f[r % 2]
                left, right, kind = PROJ[r]
                if r < 2:
                    cols = slice(COLS[left], COLS[left] + PH * XD)
                    for c in range(KC):
                        pe.matmul(bank[:], xs[par][:, kind, c, :], w_h[:, c, cols], start=(c == 0), stop=False)
                        mm = pe.matmul(bank[:], xs[par][:, kind, c, :], w_l[:, c, cols], start=False, stop=(c == KC - 1))
                elif r == 2:
                    cols = slice(COLS["kx"], COLS["kx"] + 4 * XD)
                    for c in range(KC):
                        pe.matmul(bank[:], c_h[par][:, c, :], w_h[:, c, cols], start=(c == 0), stop=False)
                        pe.matmul(bank[:], c_h[par][:, c, :], w_l[:, c, cols], start=False, stop=False)
                        mm = pe.matmul(bank[:], c_l[par][:, c, :], w_h[:, c, cols], start=False, stop=(c == KC - 1))
                else:
                    for n, name in enumerate(("k", "v")):
                        cols = slice(COLS[name], COLS[name] + 2 * XD)
                        out = bank[:, n * 2 * XD:(n + 1) * 2 * XD]
                        for c in range(KC):
                            pe.matmul(out, xs[par][:, 2 + n, c, :], w_h[:, c, cols], start=(c == 0), stop=False)
                            mm = pe.matmul(out, xs[par][:, 2 + n, c, :], w_l[:, c, cols], start=False, stop=(c == KC - 1))
                mm.then_inc(f_ready, 1)

            def turn(U, r):
                pe.wait_ge(normed_ready, 4 * U + (r + 3 if r < 2 else 6))
                pe.wait_ge(x_kept, 3 * U + r + 1)
                for h in range(PH):
                    mm = pe.transpose(bank_x[:, h * P:(h + 1) * P], normed[:, r, h, :], ident[:])
                mm.then_inc(x_ready, 1)

            def scores(U, par, s):
                q, kcol = (qT[par], 2) if s == 0 else (qxT[par], 0)
                pe.wait_ge(x_kept, 3 * U + 4)
                pe.wait_ge(exp_done, 2 * U + s + 1)
                for h in range(PH):
                    mm = pe.matmul(bank_s[s][:, h * P:(h + 1) * P], q[:, h, :], kT[par][:, kcol + h // XH, :], start=True, stop=True)
                mm.then_inc(s_ready, 1)

            def turn_p(U, s):
                pe.wait_ge(p_ready, 2 * U + s + 1)
                pe.wait_ge(pT_kept, 2 * U + s + 1)
                for h in range(PH):
                    mm = pe.transpose(bank_p[:, h * P:(h + 1) * P], probs[:, s, h, :], ident[:])
                mm.then_inc(pT_ready, 1)

            def weigh(U, par, s):
                pe.wait_ge(pT_kept, 2 * U + s + 2)
                pe.wait_ge(o_used, 2 * U + s + 1)
                vcol = 2 if s == 0 else 0
                for g in range(2):
                    mm = pe.matmul(bank_o[:, g * XH * P:(g + 1) * XH * P], vv[par][:, vcol + g, :],
                                   pT[:, s, g * XH:(g + 1) * XH, :].rearrange("p h t -> p (h t)"), start=True, stop=True)
                mm.then_inc(o_ready, 1)

            def out_product(U):
                pe.wait_ge(cat_ready, U + 1)
                pe.wait_ge(y_used, U + 1)
                for n in range(2 * PH):
                    mm = pe.matmul(bank_y[:, 0:D], catq[:, n // PH, n % PH, :], wp[:, n, :], start=(n == 0), stop=(n == 2 * PH - 1))
                mm.then_inc(y_ready, 1)

            def before(gp):
                pe.wait_ge(w_ready, 2 * gp + 3)

            def first(U0):
                for r in range(4):
                    project(U0, 0, r)
                for r in range(3):
                    turn(U0, r)

            def step(U, gp, b, tail, front, par=0):
                nxt = 1 - par
                if front:
                    project(U + 1, nxt, 0)
                    project(U + 1, nxt, 1)
                scores(U, par, 0)
                scores(U, par, 1)
                if tail:
                    out_product(U - 1)
                if front:
                    project(U + 1, nxt, 2)
                    project(U + 1, nxt, 3)
                turn_p(U, 0)
                turn_p(U, 1)
                if front:
                    turn(U + 1, 0)
                    turn(U + 1, 1)
                weigh(U, par, 0)
                weigh(U, par, 1)
                if front:
                    turn(U + 1, 2)

            units(pe, before, first, step, lambda U, b: out_product(U))



NE, TOP, EH, NCH, CH = 32, 4, 96, 16, 128
E_TILES = NE * EH // P
TILES = E_TILES + NCH * CH // P
CHUNK_SCALE = 0.05
WTILE = 2 * KC * P + D
BLK = 512
SPAN = 2
PASSES = NT // (BLK * SPAN)


def stage_c(nc, a, sem, banks, xres, small, ident):
    inner = ExitStack()

    def sb(name, shape, dt):
        return inner.enter_context(nc.sbuf_tensor("sb_" + name, shape, dt))

    def pair(name, shape, dt):
        return [sb(f"{name}{i}", shape, dt) for i in range(2)]

    stats, mean, var, half, tmp, rstd, bits = (small[n] for n in ("stats", "mean", "var", "half", "tmp", "rstd", "bits"))
    x_h, x_l = sb("x2_h", [P, KC, NT], F32R), sb("x2_l", [P, KC, NT], F32R)
    cwT = sb("cwT", [P, NT], F32R)
    z = pair("c_z", [P, D], F32)
    outT = sb("outT", [P, KC, NT], F32)
    gate, gate_h, gate_l = sb("gate", [P, KC, NE], F32), sb("gate_h", [P, KC, NE], F32R), sb("gate_l", [P, KC, NE], F32R)
    logitT = sb("logitT", [NE, NT], F32)
    names = ("logit", "prob", "key", "above", "equal", "count0", "count1")
    logit, prob, key, above, equal, count0, count1 = (sb(n, [P, NB, NE], F32) for n in names)
    top8 = sb("top8", [P, NB, 8], F32)
    rowmax, rowsum, nabove = (sb(n, [P, NB], F32) for n in ("rowmax", "rowsum", "nabove"))
    cw_high = sb("cw_high", [P, NB, 2, NE], F32R)
    cw_stack = sb("cw_stack", [P, NB, 2, 2, NE], F32)

    loaded = sem("c_loaded")
    c_dve = sem("c_dve")
    normed, turned, x_high, x_low = sem("c_normed"), sem("c_turned"), sem("c_x_high"), sem("c_x_low")
    gate_high, gate_low = sem("gate_high"), sem("gate_low")
    logitT_ready, logitT_kept, logit_ready = sem("logitT_ready"), sem("logitT_kept"), sem("logit_ready")
    shifted, exp_ready, stack_ready = sem("c_shifted"), sem("c_exp_ready"), sem("c_stack_ready")
    cwT_ready, cwT_kept = sem("cwT_ready"), sem("cwT_kept")

    with inner:
        with nc.Block() as block:

            @block.sync
            def _(sp):
                sp.dma_start(gate[:], a["gateT"].rearrange("(c p) e -> p c e", p=P)).then_inc(loaded, 16)

            @block.scalar
            def _(act):
                act.wait_ge(loaded, 16)
                act.activation(gate_h[:], gate[:], ACT.Copy).then_inc(gate_high, 1)
                with act.Fori(0, NB // 2) as i:
                    for k in range(2):
                        b = 2 * i + k
                        act.wait_ge(turned, b + 3)
                        act.activation(x_h[:, :, bass.ds(b * T, T)], banks[k][:, 0:D].rearrange("p (c t) -> p c t", c=KC),
                                       ACT.Copy).then_inc(x_high, 1)
                for n in range(NT // BLK):
                    act.wait_ge(logitT_ready, n + 1)
                    act.activation(logitT[:, n * BLK:(n + 1) * BLK], banks[2 + n][0:NE, :], ACT.Copy).then_inc(logitT_kept, 1)
                act.wait_ge(shifted, 1)
                act.activation(prob[:], prob[:], ACT.Exp).then_inc(exp_ready, 1)
                act.activation(key[:], logit[:], ACT.Exp, scale=-1.0).then_inc(exp_ready, 1)
                for n in range(NT // BLK):
                    act.wait_ge(cwT_ready, n + 1)
                    act.activation(cwT[:, n * BLK:(n + 1) * BLK], banks[2 + n][:], ACT.Copy).then_inc(cwT_kept, 1)

            @block.vector
            def _(dve):
                chain = Chain(dve, c_dve)
                link = chain.link
                dve.sem_inc(x_low, 2)
                with dve.Fori(0, NB) as b:
                    chain.enter(b, 1)
                    r = xres[:, bass.ds(b, 1), :].rearrange("p b d -> p (b d)")
                    link(dve.bn_stats(stats[:, bass.ds(b, 1), :].rearrange("p b s -> p (b s)"), r))
                    chain.leave(NB)
                mean_var_steps(dve, link, stats, mean[:], var[:], tmp[:])
                rsqrt_steps(dve, link, var[:], half[:], bits[:], tmp[:], rstd[:])
                with dve.Fori(0, NB // 2) as i:
                    for k in range(2):
                        b = 2 * i + k
                        r = xres[:, bass.ds(b, 1), :].rearrange("p b d -> p (b d)")
                        dve.wait_ge(turned, b + 1)
                        dve.tensor_scalar(z[k][:], r, mean[:, bass.ds(b, 1)], rstd[:, bass.ds(b, 1)],
                                          ALU.subtract, ALU.mult).then_inc(normed, 1)
                        dve.wait_ge(normed, b + 1)
                        dve.tensor_scalar(r, z[k][:], 1.0, None, ALU.mult)
                    for k in range(2):
                        b = 2 * i + k
                        dve.wait_ge(x_high, b + 1)
                        dve.tensor_tensor(x_l[:, :, bass.ds(b * T, T)], banks[k][:, 0:D].rearrange("p (c t) -> p c t", c=KC),
                                          x_h[:, :, bass.ds(b * T, T)].bitcast(F32), ALU.subtract).then_inc(x_low, 1)
                dve.wait_ge(gate_high, 1)
                dve.tensor_tensor(gate_l[:], gate[:], gate_h[:].bitcast(F32), ALU.subtract).then_inc(gate_low, 1)
                dve.wait_ge(logit_ready, 1)
                link(dve.tensor_copy(logit[:], banks[0][:].rearrange("p (b e) -> p b e", b=NB)))
                link(dve.tensor_reduce(rowmax[:], logit[:], AX_X, ALU.max))
                dve.tensor_tensor(prob[:], logit[:], ap_bcast(rowmax[:], 2, NE), ALU.subtract).then_inc(shifted, 1)
                dve.wait_ge(exp_ready, 2)
                link(dve.tensor_reduce(rowsum[:], prob[:], AX_X, ALU.add))
                link(dve.reciprocal(rowsum[:], rowsum[:]))
                link(dve.tensor_tensor(prob[:], prob[:], ap_bcast(rowsum[:], 2, NE), ALU.mult))
                link(dve.tensor_scalar(key[:], key[:], 1.0, None, ALU.add))
                link(dve.reciprocal(key[:], key[:]))
                for b in range(NB):
                    ins = dve.max(top8[:, b, :], key[:, b, :])
                link(ins)
                fourth = top8[:, :, TOP - 1:TOP].to_broadcast([P, NB, NE])
                dve.tensor_tensor(above[:], key[:], fourth, ALU.is_gt)
                link(dve.tensor_tensor(equal[:], key[:], fourth, ALU.is_equal))
                link(dve.tensor_reduce(nabove[:], above[:], AX_X, ALU.add))
                src, k = equal, 1
                for n in range(NE.bit_length() - 1):
                    dst = (count0, count1)[n % 2]
                    dve.tensor_copy(dst[:, :, 0:k], src[:, :, 0:k])
                    link(dve.tensor_tensor(dst[:, :, k:NE], src[:, :, k:NE], src[:, :, 0:NE - k], ALU.add))
                    src, k = dst, 2 * k
                link(dve.tensor_tensor(src[:], src[:], ap_bcast(nabove[:], 2, NE), ALU.add))
                link(dve.scalar_tensor_tensor(out=equal[:], in0=src[:], scalar=float(TOP), in1=equal[:], op0=ALU.is_le, op1=ALU.mult))
                link(dve.tensor_tensor(above[:], above[:], equal[:], ALU.add))
                link(dve.tensor_tensor(prob[:], prob[:], above[:], ALU.mult))
                link(dve.tensor_reduce(rowsum[:], prob[:], AX_X, ALU.add))
                link(dve.reciprocal(rowsum[:], rowsum[:]))
                link(dve.tensor_tensor(prob[:], prob[:], ap_bcast(rowsum[:], 2, NE), ALU.mult))
                link(dve.tensor_scalar(key[:], prob[:], CHUNK_SCALE, None, ALU.mult))
                dve.tensor_copy(cw_high[:, :, 0, :], prob[:])
                link(dve.tensor_copy(cw_high[:, :, 1, :], key[:]))
                high = cw_high[:].bitcast(F32)
                dve.tensor_copy(cw_stack[:, :, :, 0, :], high)
                dve.tensor_tensor(cw_stack[:, :, 0, 1, :], prob[:], high[:, :, 0, :], ALU.subtract)
                dve.tensor_tensor(cw_stack[:, :, 1, 1, :], key[:], high[:, :, 1, :], ALU.subtract).then_inc(stack_ready, 1)

            @block.tensor
            def _(pe):
                pe.sem_inc(turned, 2)
                with pe.Fori(0, NB // 2) as i:
                    for k in range(2):
                        b = 2 * i + k
                        pe.wait_ge(normed, b + 1)
                        pe.wait_ge(x_low, b + 1)
                        for c in range(KC):
                            mm = pe.transpose(banks[k][:, c * P:(c + 1) * P], z[k][:, c * P:(c + 1) * P], ident[:])
                        mm.then_inc(turned, 1)
                pe.wait_ge(gate_low, 1)
                pe.wait_ge(x_low, NB + 2)
                for n in range(NT // BLK):
                    blk = slice(n * BLK, (n + 1) * BLK)
                    for c in range(KC):
                        out = banks[2 + n][0:NE, :]
                        pe.matmul(out, gate_h[:, c, :], x_h[:, c, blk], start=(c == 0), stop=False)
                        pe.matmul(out, gate_l[:, c, :], x_h[:, c, blk], start=False, stop=False)
                        mm = pe.matmul(out, gate_h[:, c, :], x_l[:, c, blk], start=False, stop=(c == KC - 1))
                    mm.then_inc(logitT_ready, 1)
                pe.wait_ge(logitT_kept, NT // BLK)
                for b in range(NB):
                    mm = pe.transpose(banks[0][:, b * NE:(b + 1) * NE], logitT[:, b * T:(b + 1) * T], ident[0:NE, 0:NE])
                mm.then_inc(logit_ready, 1)
                pe.wait_ge(stack_ready, 1)
                for b in range(NB):
                    mm = pe.transpose(banks[2 + b // 4][:, b % 4 * P:(b % 4 + 1) * P],
                                      cw_stack[:, b].rearrange("p s t e -> p (s t e)"), ident[:])
                    if b % 4 == 3:
                        mm.then_inc(cwT_ready, 1)

        experts(nc, a, sem, banks, x_h, x_l, cwT, outT)
        last_norm(nc, a, sem, banks, xres, small, ident, outT)


def experts(nc, a, sem, banks, x_h, x_l, cwT, outT):
    inner = ExitStack()

    def pair(name, shape, dt):
        return [inner.enter_context(nc.sbuf_tensor(f"sb_{name}{i}", shape, dt)) for i in range(2)]

    bank_out, bank_g, bank_u, bank_c = banks[0:4], banks[4], banks[5], banks[6]
    raw, w_h, w_l = pair("e_raw", [P, WTILE + P], F32), pair("e_wh", [P, WTILE + P], F32R), pair("e_wl", [P, WTILE], F32R)
    sg, act_, act_h, act_l = pair("e_sg", [P, BLK], F32), pair("e_a", [P, BLK], F32), pair("e_ah", [P, BLK], F32R), pair("e_al", [P, BLK], F32R)

    w_loaded = [sem(f"e_loaded{i}") for i in range(2)]
    w_high, w_ready, tile_done = sem("e_w_high"), sem("e_w_ready"), sem("e_tile_done")
    pool_turn = sem("e_pool_turn")
    g_ready, u_ready, c_ready = sem("g_ready"), sem("u_ready"), sem("c_ready")
    silu_ready, gated, weighted, a_high, a_low = (sem(n) for n in ("silu_ready", "gated", "weighted", "a_high", "a_low"))
    out_ready, out_kept = sem("e_out_ready"), sem("e_out_kept")
    HALFT = TILES // 2

    with inner, nc.Block() as block:

        @block.sync
        def _(sp):
            sp.sem_inc(w_ready, 2)
            with sp.Fori(0, PASSES) as th:
                with sp.Fori(0, HALFT) as i:
                    for k in range(2):
                        sp.wait_ge(w_ready, th * TILES + 2 * i + k + 1)
                        sp.dma_start(raw[k][:, 0:WTILE], a["w_tiles"][bass.ds(2 * i + k, 1)].rearrange("a p n -> (a p) n")).then_inc(w_loaded[k], 16)
                        sp.dma_start(raw[k][:, WTILE:WTILE + P], a["sel_tiles"][bass.ds(2 * i + k, 1)].rearrange("a p n -> (a p) n")).then_inc(w_loaded[k], 16)

        @block.gpsimd
        def _(pool):
            pool.sem_inc(tile_done, 2)
            with pool.Fori(0, PASSES) as th:
                with pool.Fori(0, HALFT) as i:
                    for k in range(2):
                        n = th * TILES + 2 * i + k
                        pool.wait_ge(tile_done, n + 1)
                        pool.sem_inc(pool_turn, 1)
                        pool.wait_ge(w_loaded[k], (th * HALFT + i) * 32 + 32)
                        pool.sem_inc(pool_turn, 1)
                        pool.tensor_copy(w_h[k][:], raw[k][:]).then_inc(w_high, 1)
                        pool.wait_ge(w_high, n + 1)
                        pool.sem_inc(pool_turn, 1)
                        pool.tensor_tensor(w_l[k][:], raw[k][:, 0:WTILE], w_h[k][:, 0:WTILE].bitcast(F32),
                                           ALU.subtract).then_inc(w_ready, 1)

        @block.scalar
        def _(act):
            act.sem_inc(silu_ready, 1)
            act.sem_inc(out_kept, 1)
            with act.Fori(0, PASSES) as th:
                with act.Fori(0, TILES) as t:
                    for s in range(SPAN):
                        q = (th * TILES + t) * SPAN + s
                        act.wait_ge(g_ready, q + 1)
                        act.activation(sg[s][:], bank_g[:], ACT.Silu).then_inc(silu_ready, 1)
                        act.wait_ge(weighted, q + 2)
                        act.activation(act_h[s][:], act_[s][:], ACT.Copy).then_inc(a_high, 1)
                act.wait_ge(out_ready, th + 1)
                for c in range(KC):
                    for s in range(SPAN):
                        ins = act.activation(outT[:, c, bass.ds(th * (SPAN * BLK) + s * BLK, BLK)], bank_out[c * SPAN + s][:], ACT.Copy)
                ins.then_inc(out_kept, 1)

        @block.vector
        def _(dve):
            dve.sem_inc(gated, 1)
            dve.sem_inc(weighted, 1)
            with dve.Fori(0, PASSES) as th:
                with dve.Fori(0, TILES) as t:
                    for s in range(SPAN):
                        q = (th * TILES + t) * SPAN + s
                        dve.wait_ge(silu_ready, q + 2)
                        dve.wait_ge(u_ready, q + 1)
                        dve.tensor_tensor(sg[s][:], sg[s][:], bank_u[:], ALU.mult).then_inc(gated, 1)
                        dve.wait_ge(gated, q + 2)
                        dve.wait_ge(c_ready, q + 1)
                        dve.tensor_tensor(act_[s][:], sg[s][:], bank_c[:], ALU.mult).then_inc(weighted, 1)
                        dve.wait_ge(a_high, q + 1)
                        dve.tensor_tensor(act_l[s][:], act_[s][:], act_h[s][:].bitcast(F32), ALU.subtract).then_inc(a_low, 1)

        @block.tensor
        def _(pe):
            def three(out, left_h, left_l, right_h, right_l, start, stop):
                pe.matmul(out, left_h, right_h, start=start, stop=False)
                pe.matmul(out, left_l, right_h, start=False, stop=False)
                return pe.matmul(out, left_h, right_l, start=False, stop=stop)

            def up(th, n, q, k, s):
                blk = bass.ds(th * (SPAN * BLK) + s * BLK, BLK)
                if s == 0:
                    pe.wait_ge(w_ready, n + 3)
                for m, (bank, ready) in enumerate(((bank_g, g_ready), (bank_u, u_ready))):
                    pe.wait_ge((silu_ready, gated)[m], q + 1)
                    for c in range(KC):
                        col = slice((m * KC + c) * P, (m * KC + c + 1) * P)
                        mm = three(bank[:], w_h[k][:, col], w_l[k][:, col], x_h[:, c, blk], x_l[:, c, blk], c == 0, c == KC - 1)
                    mm.then_inc(ready, 1)
                pe.wait_ge(weighted, q + 1)
                pe.matmul(bank_c[:], w_h[k][:, WTILE:WTILE + P], cwT[:, blk], start=True, stop=True).then_inc(c_ready, 1)

            def down(q, k, s, first, last):
                pe.wait_ge(a_low, q + 1)
                for c in range(KC):
                    col = slice(2 * KC * P + c * P, 2 * KC * P + (c + 1) * P)
                    mm = three(bank_out[c * SPAN + s][:], w_h[k][:, col], w_l[k][:, col], act_h[s][:], act_l[s][:], first, last)
                if s == SPAN - 1:
                    mm.then_inc(tile_done, 1)
                return mm

            with pe.Fori(0, PASSES) as th:
                n0, q0 = th * TILES, th * TILES * SPAN

                def tile(t, k, first=False, last=False):
                    q = q0 + t * SPAN
                    up(th, n0 + t, q + 1, k, 1)
                    down(q, k, 0, first, last)
                    if not last:
                        up(th, n0 + t + 1, q + 2, 1 - k, 0)
                    return down(q + 1, k, 1, first, last)

                up(th, n0, q0, 0, 0)
                pe.wait_ge(out_kept, th + 1)
                tile(0, 0, first=True)
                with pe.Fori(0, HALFT - 1) as i:
                    tile(2 * i + 1, 1)
                    tile(2 * i + 2, 0)
                tile(TILES - 1, 1, last=True)
                pe.wait_ge(tile_done, n0 + TILES + 2)
                pe.sem_inc(out_ready, 1)


def last_norm(nc, a, sem, banks, xres, small, ident, outT):
    stats, mean, var, half, tmp, rstd, bits = (small[n] for n in ("stats", "mean", "var", "half", "tmp", "rstd", "bits"))
    turned, added, normed, written, n_dve = (sem("n_" + n) for n in ("turned", "added", "normed", "written", "dve"))
    outT_s = sem("n_staged")

    with ExitStack() as inner, nc.Block() as block:
        stage = [inner.enter_context(nc.sbuf_tensor(f"sb_n_stage{i}", [P, KC, T], F32)) for i in range(2)]

        @block.scalar
        def _(act):
            with act.Fori(0, NB // 2) as i:
                for k in range(2):
                    b = 2 * i + k
                    act.wait_ge(turned, b + 1)
                    act.activation(stage[k][:], outT[:, :, bass.ds(b * T, T)], ACT.Copy).then_inc(outT_s, 1)

        @block.tensor
        def _(pe):
            pe.sem_inc(turned, 2)
            with pe.Fori(0, NB // 2) as i:
                for k in range(2):
                    b = 2 * i + k
                    pe.wait_ge(outT_s, b + 1)
                    pe.wait_ge(added, b + 1)
                    for c in range(KC):
                        mm = pe.transpose(banks[k][:, c * P:(c + 1) * P], stage[k][:, c, :], ident[:])
                    mm.then_inc(turned, 1)

        @block.vector
        def _(dve):
            chain = Chain(dve, n_dve)
            link = chain.link
            dve.sem_inc(added, 2)
            with dve.Fori(0, NB // 2) as i:
                chain.enter(i, 2)
                for k in range(2):
                    b = 2 * i + k
                    r = xres[:, bass.ds(b, 1), :].rearrange("p b d -> p (b d)")
                    dve.wait_ge(turned, b + 3)
                    dve.tensor_tensor(r, r, banks[k][:, 0:D], ALU.add).then_inc(added, 1)
                    dve.wait_ge(added, b + 3)
                    link(dve.bn_stats(stats[:, bass.ds(b, 1), :].rearrange("p b s -> p (b s)"), r))
                chain.leave(NB // 2)
            mean_var_steps(dve, link, stats, mean[:], var[:], tmp[:])
            rsqrt_steps(dve, link, var[:], half[:], bits[:], tmp[:], rstd[:])
            with dve.Fori(0, NB) as b:
                r = xres[:, bass.ds(b, 1), :].rearrange("p b d -> p (b d)")
                dve.tensor_scalar(r, r, mean[:, bass.ds(b, 1)], rstd[:, bass.ds(b, 1)],
                                  ALU.subtract, ALU.mult).then_inc(normed, 1)

        @block.sync
        def _(sp):
            for n in range(4):
                bs = slice(n * NB // 4, (n + 1) * NB // 4)
                sp.wait_ge(normed, (n + 1) * NB // 4)
                sp.dma_start(a["out"][bs].rearrange("b t d -> t b d"), xres[:, bs, :]).then_inc(written, 16)
            sp.wait_ge(written, 16 * 4)


def layout(inputs):
    import numpy as np

    x = np.asarray(inputs["x"])
    wq, wk, wv = (np.asarray(inputs[f"L0_attn_W{c}"]) for c in "qkv")
    bq, bk, bv = (np.asarray(inputs[f"L0_attn_b{c}"]) for c in "qkv")
    order = np.arange(D).reshape(2, HALF, G, HD).transpose(0, 2, 1, 3).reshape(D)
    out = {
        "x": x,
        "xT": x.reshape(NT, D).T,
        "w_qkvT": np.concatenate([wq[order], wk, wv]).T,
        "b_qkv": np.concatenate([bq[order], bk, bv])[None],
        "w_oT": np.asarray(inputs["L0_attn_Wo"]).T,
        "b_o": np.asarray(inputs["L0_attn_bo"])[None],
    }
    x8 = "L0_xattn_"
    get = lambda n: np.asarray(inputs[x8 + n])
    out["ctxT"] = np.asarray(inputs["ctx_2048"]).reshape(NT, D).T
    out["ln_wb"] = np.stack([get("ln_w"), get("ln_b")]).reshape(2, KC, P).transpose(2, 0, 1)
    out["in_scale"] = np.stack([get(f"{n}_in_scale") for n in ("q", "qx", "k", "v")]).reshape(KINDS, KC, P).transpose(2, 0, 1)
    out["w_scale"] = np.stack([get(f"{n}_scale") for n in ("wq", "wqx", "wk", "wv")])[None]
    out["out_scale"] = np.stack([get("proj_in_scale"), get("proj_w_scale")])[None]
    out["smooth"] = get("proj_smooth").reshape(2, XG * XH, XD).transpose(2, 0, 1)
    out["norm_w"] = np.stack([get(f"{n}ln_w") for n in ("q", "qx", "kx", "k")], 1)
    out["norm_b"] = np.stack([get(f"{n}ln_b") for n in ("q", "qx", "kx", "k")], 1)
    kvx = get("w_kv_x")
    parts = [get("wq"), get("wqx"), kvx[:XG * XD], kvx[XG * XD:], get("wk"), get("wv")]
    out["w_pairs"] = np.concatenate([w.reshape(PAIRS, -1, D) for w in parts], 1).transpose(0, 2, 1)
    proj = get("wproj").T.reshape(2, PAIRS, PH, XD, D)
    out["wproj_pairs"] = proj.transpose(1, 0, 2, 3, 4).reshape(PAIRS, 2 * PH, XD, D)
    f8 = "L0_ffn_"
    out["gateT"] = np.asarray(inputs[f8 + "gate_w"]).T
    tiles = []
    for large, chunk in (("Wg", "cWg"), ("Wu", "cWu")):
        for n, count in ((large, NE * EH), (chunk, NCH * CH)):
            w = np.asarray(inputs[f8 + n]).transpose(1, 0, 2).reshape(KC, P, count // P, P)
            tiles.append(w.transpose(2, 1, 0, 3).reshape(count // P, P, KC * P))
    down = [np.asarray(inputs[f8 + n]).reshape(-1, P, D) for n in ("Wd", "cWd")]
    out["w_tiles"] = np.concatenate([np.concatenate([tiles[0], tiles[2], down[0]], 2),
                                     np.concatenate([tiles[1], tiles[3], down[1]], 2)])
    f = np.float32
    inv = f(1.0) / f(10000.0) ** (np.arange(0, HD, 2, dtype=f) / f(HD))
    ang = np.arange(T, dtype=f)[:, None] * inv[None]
    cos, sin = np.cos(ang), np.sin(ang)
    out["rope"] = np.stack([np.concatenate([cos, cos], 1), np.concatenate([-sin, sin], 1)], 1)
    out["ident"] = np.eye(P, dtype=f)
    rows = np.arange(STACK) % (HALF * HD) // HD
    out["gmask"] = (rows[:, None] == np.arange(HALF)[None]).astype(f)
    sel = np.zeros((TILES, 2, 2, NE, P), f)
    for t in range(TILES):
        for i in range(P):
            if t < E_TILES:
                sel[t, 0, :, (t * P + i) // EH, i] = 1
            else:
                c = ((t - E_TILES) * P + i) // CH
                sel[t, 1, :, c * NE // NCH:(c + 1) * NE // NCH, i] = 1
    out["sel_tiles"] = sel.reshape(TILES, P, P)
    return {n: np.ascontiguousarray(v) for n, v in out.items()}


def kernel(**inputs):
    import concourse.bacc as bacc
    from concourse.bass_utils import run_bass_kernel_spmd

    nc = bacc.Bacc("TRN2", target_bir_lowering=False, num_devices=1)
    arrays = layout(inputs)
    args = {n: nc.dram_tensor(n, v.shape, mybir.dt.from_np(v.dtype), kind="ExternalInput").ap() for n, v in arrays.items()}
    args["out"] = nc.dram_tensor("out", (NB, T, D), F32, kind="ExternalOutput").ap()
    program(nc, args)
    return run_bass_kernel_spmd(nc, [arrays], core_ids=[0]).results[0]["out"]
```

```python
from contextlib import ExitStack

import concourse.bass as bass
from concourse import mybir

ALU = mybir.AluOpType
ACT = mybir.ActivationFunctionType
F32 = mybir.dt.float32
F32R = mybir.dt.float32r
BF16 = mybir.dt.bfloat16
U16 = mybir.dt.uint16
I32 = mybir.dt.int32
AX_X = mybir.AxisListType.X

P = 128
NB = 16
T = 128
NT = NB * T
D = 256
KC = D // P
EPS = 1e-5

HKV, G, HD = 8, 4, 8
QKV = D + 2 * HKV * HD
TERMS = 3
HALF = HKV // 2
STACK = TERMS * HALF * HD
PVW = HKV * HD + HKV
TURNS = 4


def ap_bcast(ap, axis, n):
    a = ap.unsqueeze(axis)
    shape = list(a.shape)
    shape[axis] = n
    return a.to_broadcast(shape)


def rsqrt_steps(dve, link, var, half, bits, tmp, y):
    link(dve.tensor_scalar(half, var, -0.5, None, ALU.mult))
    link(dve.tensor_scalar(bits, var.bitcast(I32), 1, None, ALU.logical_shift_right))
    link(dve.tensor_scalar(y.bitcast(I32), bits, -1.0, float(0x5F3759DF), ALU.mult, ALU.add))
    for _ in range(3):
        link(dve.tensor_tensor(tmp, y, y, ALU.mult))
        link(dve.tensor_tensor(tmp, tmp, half, ALU.mult))
        link(dve.scalar_tensor_tensor(out=y, in0=tmp, scalar=1.5, in1=y, op0=ALU.add, op1=ALU.mult))


RSQRT_LINKS = 12


def mean_var_steps(dve, link, stats, mean, var, tmp):
    m0, m1 = stats[:, :, 1], stats[:, :, 4]
    link(dve.tensor_tensor(mean, m0, m1, ALU.add))
    link(dve.tensor_scalar(mean, mean, 0.5, None, ALU.mult))
    link(dve.tensor_tensor(tmp, m0, m1, ALU.subtract))
    link(dve.scalar_tensor_tensor(out=tmp, in0=tmp, scalar=0.25, in1=tmp, op0=ALU.mult, op1=ALU.mult))
    link(dve.tensor_tensor(var, stats[:, :, 2], stats[:, :, 5], ALU.add))
    link(dve.scalar_tensor_tensor(out=var, in0=var, scalar=1.0 / D, in1=tmp, op0=ALU.mult, op1=ALU.add))
    link(dve.tensor_scalar(var, var, EPS, None, ALU.add))


class Chain:

    def __init__(self, eng, sem):
        self.eng, self.sem, self.base, self.n, self.done, self.loops = eng, sem, 0, 0, 0, []

    def link(self, ins):
        ins.then_inc(self.sem, 1)
        self.n += 1
        self.done += 1
        self.eng.wait_ge(self.sem, self.base + self.n)

    def enter(self, i, per):
        start = self.base + self.n
        self.loops.append((start, per, self.done))
        self.base, self.n, self.done = start + i * per, 0, 0

    def leave(self, rounds):
        start, per, done = self.loops.pop()
        assert self.done == per, (self.done, per)
        self.base, self.n, self.done = start + rounds * per, 0, done + rounds * per


def program(nc, a):
    with ExitStack() as ctx:
        build(nc, a, ctx)


def build(nc, a, ctx):
    def sb(name, shape, dt):
        return ctx.enter_context(nc.sbuf_tensor("sb_" + name, shape, dt))

    def sem(name):
        return ctx.enter_context(nc.semaphore(name))

    banks = [ctx.enter_context(nc.psum_tensor(f"bank{i}", [P, 512], F32)) for i in range(8)]

    xres = sb("xres", [P, NB, D], F32)
    stats = sb("stats", [P, NB, 6], F32)
    mean, var, half, tmp, rstd = (sb(n, [P, NB], F32) for n in ("mean", "var", "half", "tmp", "rstd"))
    bits = sb("bits", [P, NB], I32)
    ident = sb("ident", [P, P], F32)

    small = dict(stats=stats, mean=mean, var=var, half=half, tmp=tmp, rstd=rstd, bits=bits)

    stage_a(nc, a, sem, banks, xres, stats, ident)
    with ExitStack() as mid:
        xq = mid.enter_context(nc.sbuf_tensor("sb_xq", [P, KINDS, KC, NT + T], BF16))
        ahead = LoadsOfB(nc, a, sem, mid)
        stage_l(nc, a, sem, banks, xres, small, ident, xq, ahead)
        stage_b(nc, a, sem, banks, xres, ident, xq, ahead)
    stage_c(nc, a, sem, banks, xres, small, ident)


def stage_a(nc, a, sem, banks, xres, stats, ident):
    inner = ExitStack()

    def sb(name, shape, dt):
        return inner.enter_context(nc.sbuf_tensor("sb_" + name, shape, dt))

    bank_qkv, bank_stack, bank_s0, bank_s1, bank_p0, bank_p1, bank_o, bank_y = banks
    bank_s, bank_p = (bank_s0, bank_s1), (bank_p0, bank_p1)

    xT = sb("xT", [P, KC, NT + T], F32)
    w_qkv = sb("w_qkv", [P, KC, QKV], F32)
    w_qkv_h, w_qkv_l = sb("w_qkv_h", [P, KC, QKV], F32R), sb("w_qkv_l", [P, KC, QKV], F32R)
    w_o = sb("w_o", [P, KC, D], F32)
    w_o_h, w_o_l = sb("w_o_h", [P, KC, D], F32R), sb("w_o_l", [P, KC, D], F32R)
    b_qkv, b_o = sb("b_qkv", [P, QKV], F32), sb("b_o", [P, D], F32)
    rope = sb("rope", [P, 2, HD], F32)
    gmask = sb("gmask", [STACK, HALF], F32)
    xh = [sb(f"xh{i}", [P, KC, P], F32R) for i in range(2)]
    xl = [sb(f"xl{i}", [P, KC, P], F32R) for i in range(2)]
    qkv = sb("qkv", [P, QKV], F32)
    rot = sb("rot", [P, QKV - HKV * HD], F32)
    q_stack = sb("q_stack", [P, 2 * G, TERMS, HALF * HD], F32R)
    k_stack = sb("k_stack", [P, 2, TERMS, HALF * HD], F32R)
    qT = [sb(f"qT{i}", [STACK, 2 * G, P], F32R) for i in range(2)]
    kbd = [sb(f"kbd{i}", [STACK, 2, HALF, P], F32R) for i in range(2)]
    v_h = [sb(f"v_h{i}", [P, (HKV + 1) * PVW], F32R) for i in range(2)]
    v_l = [sb(f"v_l{i}", [P, (HKV + 1) * PVW], F32R) for i in range(2)]
    smax = [sb(f"smax{i}", [P, HALF], F32) for i in range(2)]
    probs = [sb(f"probs{i}", [P, HALF, P], F32) for i in range(4)]
    pT_h = [sb(f"pT_h{i}", [P, HALF, G, P], F32R) for i in range(4)]
    pT_l = [sb(f"pT_l{i}", [P, HALF, G, P], F32R) for i in range(4)]
    oT = sb("oT", [PVW, G, P], F32)
    rsum = sb("rsum", [P, G, HKV], F32)
    attn = sb("attn", [P, HKV, G, HD], F32)
    aT_h, aT_l = sb("aT_h", [P, KC, P], F32R), sb("aT_l", [P, KC, P], F32R)

    loaded, rest_loaded = sem("a_loaded"), sem("a_rest_loaded")
    w_high, w_low = sem("a_w_high"), sem("a_w_low")
    zeroed = sem("a_zeroed")
    x_h, x_l = sem("a_x_h"), sem("a_x_l")
    qkv_ready, qkv_used = sem("qkv_ready"), sem("qkv_used")
    stacked = sem("stacked")
    stackT_ready, stackT_used = sem("stackT_ready"), sem("stackT_used")
    v_ready, k_ready = sem("v_ready"), sem("k_ready")
    s_ready = sem("s_ready")
    max_ready, p_ready = sem("a_max_ready"), sem("p_ready")
    swapped, turned, biased = sem("swapped"), sem("turned"), sem("a_biased")
    rotated, stack_high, v_high, pool_turn = sem("rotated"), sem("stack_high"), sem("v_high"), sem("a_pool_turn")
    w_scaled, x_padded = sem("w_scaled"), sem("x_padded")
    pT_ready, pT_high, pT_low = sem("pT_ready"), sem("pT_high"), sem("pT_low")
    pv_done = sem("pv_done")
    oT_kept = sem("oT_kept")
    o_ready, attn_ready = sem("o_ready"), sem("attn_ready")
    aT_ready, aT_high, aT_low = sem("aT_ready"), sem("aT_high"), sem("aT_low")
    y_ready, y_used = sem("y_ready"), sem("y_used")
    a_dve = sem("a_dve")

    NLOAD = 8
    WEIGH_SAME, WEIGH_NEXT = {4: (0,), 5: (1,), 6: (2,), 7: (3,)}, {0: (4, 5), 1: (6, 7)}

    def batches(eng, first, step, chain=None, per=0):
        first()
        step(0, 0, False, True)
        with eng.Fori(0, (NB - 2) // 2) as i:
            if chain:
                chain.enter(i, per)
            for k in (1, 2):
                step(2 * i + k, k % 2, True, True)
            if chain:
                chain.leave((NB - 2) // 2)
        step(NB - 1, 1, True, False)

    def early(b, n=1):
        return isinstance(b, int) and b < n

    with inner, nc.Block() as block:

        @block.sync
        def _(sp):
            first, rest = slice(0, 2 * T), slice(2 * T, NT)
            src = a["xT"].rearrange("(c p) t -> p c t", p=P)
            sp.dma_start(xT[:, :, first], src[:, :, first]).then_inc(loaded, 16)
            sp.dma_start(w_qkv[:], a["w_qkvT"].rearrange("(c p) n -> p c n", p=P)).then_inc(loaded, 16)
            sp.dma_start(b_qkv[:], a["b_qkv"].to_broadcast([P, QKV])).then_inc(loaded, 16)
            sp.dma_start(rope[:], a["rope"]).then_inc(loaded, 16)
            sp.dma_start(ident[:], a["ident"]).then_inc(loaded, 16)
            sp.dma_start(gmask[:], a["gmask"]).then_inc(loaded, 16)
            sp.dma_start(w_o[:], a["w_oT"].rearrange("(c p) n -> p c n", p=P)).then_inc(loaded, 16)
            sp.dma_start(b_o[:], a["b_o"].to_broadcast([P, D])).then_inc(loaded, 16)
            sp.dma_start(xT[:, :, rest], src[:, :, rest]).then_inc(rest_loaded, 16)
            sp.dma_start(xres[:], a["x"].rearrange("b t d -> t b d")).then_inc(rest_loaded, 16)

        @block.scalar
        def _(act):
            act.wait_ge(loaded, 16 * NLOAD)
            act.wait_ge(w_scaled, 2)
            act.wait_ge(x_padded, 1)
            act.activation(w_qkv_h[:], w_qkv[:], ACT.Copy).then_inc(w_high, 1)
            act.activation(w_o_h[:], w_o[:], ACT.Copy).then_inc(w_high, 1)

            def split_x(b, par):
                if not early(b, 2):
                    act.wait_ge(qkv_ready, b - 1)
                    act.wait_ge(rest_loaded, 32)
                act.activation(xh[par][:], xT[:, :, bass.ds(b * T, T)], ACT.Copy).then_inc(x_h, 1)

            def keep_qT(b, par, r):
                act.wait_ge(stackT_ready, 3 * b + r + 1)
                if not early(b, 2):
                    act.wait_ge(s_ready, 8 * (b - 1))
                act.activation(qT[par][:, r * G:(r + 1) * G, :],
                               bank_stack[0:STACK, :].rearrange("p (j t) -> p j t", j=G),
                               ACT.Copy).then_inc(stackT_used, 1)

            def exps(b, n):
                act.wait_ge(max_ready, 8 * b + n + 1)
                if not (early(b) and n < 4):
                    act.wait_ge(pT_ready, 8 * b + n - 3)
                for g in range(HALF):
                    ins = act.activation(probs[n % 4][:, g, :], bank_s[n % 2][:, g * P:(g + 1) * P], ACT.Exp,
                                         bias=smax[n % 2][:, g:g + 1])
                ins.then_inc(p_ready, 1)

            def high(b, par, n):
                h = 2 * par + n // G
                act.wait_ge(pT_ready, 8 * b + n + 1)
                if not early(b):
                    act.wait_ge(pv_done, HKV * (b - 1) + HALF * (n // G + 1))
                act.activation(pT_h[h][:, :, n % G, :], bank_p[n % 2][:].rearrange("p (g t) -> p g t", g=HALF),
                               ACT.Copy).then_inc(pT_high, 1)

            def keep_oT(b):
                act.wait_ge(pv_done, HKV * (b + 2))
                act.activation(oT[:].rearrange("p j t -> p (j t)"), bank_o[0:PVW, :], ACT.Copy).then_inc(oT_kept, 1)

            def keep_aT(b):
                act.wait_ge(aT_ready, b + 1)
                act.activation(aT_h[:], bank_y[:, 0:D].rearrange("p (c t) -> p c t", c=KC), ACT.Copy).then_inc(aT_high, 1)

            def first():
                split_x(0, 0)
                split_x(1, 1)
                keep_qT(0, 0, 0)
                keep_qT(0, 0, 1)
                exps(0, 0)
                exps(0, 1)

            def step(b, par, tail, front):
                for n in range(8):
                    if n in (1, 3) and front:
                        keep_qT(b + 1, 1 - par, n // 2)
                    high(b, par, n)
                    if n == 2 and tail:
                        keep_oT(b - 1)
                    if n == 0 and front:
                        split_x(b + 2, par)
                    if n < 6:
                        exps(b, n + 2)
                    elif front:
                        exps(b + 1, n - 6)
                    if n == 5 and tail:
                        keep_aT(b - 1)

            batches(act, first, step)
            keep_oT(NB - 1)
            keep_aT(NB - 1)

        @block.gpsimd
        def _(pool):
            for i in range(2):
                pool.memset(v_h[i][:].bitcast(F32), 0.0).then_inc(zeroed, 1)
                pool.memset(v_l[i][:].bitcast(F32), 0.0).then_inc(zeroed, 1)
            pool.wait_ge(zeroed, 4)
            for i in range(2):
                ones = v_h[i][:, HKV * HD:HKV * HD + HKV * (PVW + 1)]
                ones = ones.rearrange("p (g c) -> p g c", g=HKV)[:, :, 0]
                pool.memset(ones.bitcast(F32), 1.0).then_inc(zeroed, 1)
            pool.memset(xT[:, :, NT:NT + T], 0.0).then_inc(x_padded, 1)
            pool.wait_ge(zeroed, 6)

            def stack(b, par):
                heads = (QKV - HKV * HD) // HD
                src = qkv[:, 0:heads * HD].rearrange("p (h d) -> p h d", d=HD)
                dst = rot[:].rearrange("p (h d) -> p h d", d=HD)
                hh = HD // 2
                pool.wait_ge(qkv_used, b + 1)
                pool.sem_inc(pool_turn, 1)
                pool.tensor_tensor(dst[:, :, 0:hh], src[:, :, hh:HD], ap_bcast(rope[:, 1, 0:hh], 1, heads), ALU.mult)
                pool.tensor_tensor(dst[:, :, hh:HD], src[:, :, 0:hh], ap_bcast(rope[:, 1, hh:HD], 1, heads),
                                   ALU.mult).then_inc(swapped, 1)
                pool.wait_ge(swapped, b + 1)
                pool.sem_inc(pool_turn, 1)
                pool.tensor_tensor(src, src, ap_bcast(rope[:, 0, :], 1, heads), ALU.mult).then_inc(turned, 1)
                pool.wait_ge(turned, b + 1)
                pool.sem_inc(pool_turn, 1)
                pool.tensor_tensor(rot[:], rot[:], qkv[:, 0:heads * HD], ALU.add).then_inc(rotated, 1)
                q = rot[:, 0:D].rearrange("p (j c) -> p j c", j=2 * G)
                k = rot[:, D:D + HKV * HD].rearrange("p (h c) -> p h c", h=2)
                if not early(b):
                    pool.wait_ge(stackT_ready, 3 * b)
                pool.wait_ge(rotated, b + 1)
                pool.sem_inc(pool_turn, 1)
                pool.tensor_copy(q_stack[:, :, 0, :], q)
                pool.tensor_copy(k_stack[:, :, 0, :], k)
                pool.tensor_copy(q_stack[:, :, 1, :], q)
                pool.tensor_copy(k_stack[:, :, 2, :], k).then_inc(stack_high, 1)
                pool.wait_ge(stack_high, b + 1)
                pool.tensor_tensor(q_stack[:, :, 2, :], q, q_stack[:, :, 0, :].bitcast(F32), ALU.subtract)
                pool.tensor_tensor(k_stack[:, :, 1, :], k, k_stack[:, :, 0, :].bitcast(F32),
                                   ALU.subtract).then_inc(stacked, 1)
                v = qkv[:, D + HKV * HD:QKV].rearrange("p (g d) -> p g d", g=HKV)
                gap = PVW + HD
                vh = v_h[par][:, 0:HKV * gap].rearrange("p (g c) -> p g c", g=HKV)[:, :, 0:HD]
                vl = v_l[par][:, 0:HKV * gap].rearrange("p (g c) -> p g c", g=HKV)[:, :, 0:HD]
                if not early(b, 2):
                    pool.wait_ge(pv_done, HKV * b)
                    pool.sem_inc(pool_turn, 1)
                pool.tensor_copy(vh, v).then_inc(v_high, 1)
                pool.wait_ge(v_high, b + 1)
                pool.tensor_tensor(vl, v, vh.bitcast(F32), ALU.subtract).then_inc(v_ready, 1)

            pool.wait_ge(loaded, 16 * NLOAD)

            def first():
                stack(0, 0)
                pool.wait_ge(rest_loaded, 32)
                pool.tensor_tensor(xres[:], xres[:], ap_bcast(b_o[:], 1, NB), ALU.add).then_inc(biased, 1)
                stack(1, 1)

            batches(pool, first,
                    lambda b, par, tail, front: stack(b + 2, par) if front else None)

        @block.vector
        def _(dve):
            chain = Chain(dve, a_dve)
            link = chain.link
            dve.sem_inc(y_used, 1)
            dve.wait_ge(loaded, 16 * NLOAD)
            for t in (w_qkv[:, :, 0:D], b_qkv[:, 0:D]):
                dve.tensor_scalar(t, t, float(HD) ** -0.5, None, ALU.mult).then_inc(w_scaled, 1)
            dve.wait_ge(w_scaled, 2)
            dve.wait_ge(w_high, 2)
            dve.tensor_tensor(w_qkv_l[:], w_qkv[:], w_qkv_h[:].bitcast(F32), ALU.subtract).then_inc(w_low, 1)
            dve.tensor_tensor(w_o_l[:], w_o[:], w_o_h[:].bitcast(F32), ALU.subtract).then_inc(w_low, 1)
            dve.wait_ge(x_padded, 1)

            def split_x(b, par):
                dve.wait_ge(x_h, b + 1)
                dve.tensor_tensor(xl[par][:], xT[:, :, bass.ds(b * P, P)], xh[par][:].bitcast(F32),
                                  ALU.subtract).then_inc(x_l, 1)

            def bias(b):
                dve.wait_ge(qkv_ready, b + 1)
                if not early(b):
                    dve.wait_ge(v_ready, b)
                dve.tensor_tensor(qkv[:], bank_qkv[:, 0:QKV], b_qkv[:], ALU.add).then_inc(qkv_used, 1)

            def spread_k(b, par):
                dve.wait_ge(stackT_ready, 3 * b + 3)
                if not early(b, 2):
                    dve.wait_ge(s_ready, 8 * (b - 1))
                for h in range(2):
                    src = ap_bcast(bank_stack[0:STACK, h * P:(h + 1) * P], 1, HALF)
                    ins = dve.tensor_tensor(kbd[par][:, h], src, ap_bcast(gmask[:], 2, P), ALU.mult)
                ins.then_inc(stackT_used, 1)

            def maxima(b, n):
                dve.wait_ge(s_ready, 8 * b + n + 1)
                dve.tensor_reduce(smax[n % 2][:], bank_s[n % 2][:].rearrange("p (g k) -> p g k", g=HALF),
                                  AX_X, ALU.max, negate=True).then_inc(max_ready, 1)

            def low(b, par, n):
                h = 2 * par + n // G
                dve.wait_ge(pT_high, 8 * b + n + 1)
                dve.tensor_tensor(pT_l[h][:, :, n % G, :], bank_p[n % 2][:].rearrange("p (g t) -> p g t", g=HALF),
                                  pT_h[h][:, :, n % G, :].bitcast(F32), ALU.subtract).then_inc(pT_low, 1)

            def normalise(b):
                dve.wait_ge(o_ready, b + 1)
                o3 = bank_y[:, 0:G * PVW].rearrange("p (j c) -> p j c", j=G)
                link(dve.reciprocal(rsum[:], o3[:, :, HKV * HD:PVW]))
                for j in range(G):
                    ins = dve.tensor_tensor(attn[:, :, j, :], o3[:, j, 0:HKV * HD].rearrange("p (g d) -> p g d", g=HKV),
                                            ap_bcast(rsum[:, j, :], 2, HD), ALU.mult)
                ins.then_inc(attn_ready, 1)

            def low_a(b):
                dve.wait_ge(aT_high, b + 1)
                dve.tensor_tensor(aT_l[:], bank_y[:, 0:D].rearrange("p (c t) -> p c t", c=KC),
                                  aT_h[:].bitcast(F32), ALU.subtract).then_inc(aT_low, 1)

            def residual(b):
                dve.wait_ge(y_ready, b + 1)
                if early(b):
                    dve.wait_ge(biased, 1)
                r = xres[:, bass.ds(b, 1), :]
                dve.tensor_tensor(r, r, bank_y[:, 0:D].unsqueeze(1), ALU.add).then_inc(y_used, 1)
                dve.wait_ge(y_used, b + 2)
                link(dve.bn_stats(stats[:, bass.ds(b, 1), :].rearrange("p b s -> p (b s)"), r.rearrange("p b d -> p (b d)")))

            def first():
                split_x(0, 0)
                split_x(1, 1)
                bias(0)
                bias(1)
                spread_k(0, 0)
                maxima(0, 0)
                maxima(0, 1)

            def step(b, par, tail, front):
                for n in range(8):
                    if n == 5 and front:
                        spread_k(b + 1, 1 - par)
                    if n < 6:
                        maxima(b, n + 2)
                    elif front:
                        maxima(b + 1, n - 6)
                    low(b, par, n)
                    if n == 0 and front:
                        split_x(b + 2, par)
                    if n == 2 and front:
                        bias(b + 2)
                    if n == 4 and tail:
                        normalise(b - 1)
                    if n == 6 and tail:
                        low_a(b - 1)
                    if n == 7 and tail:
                        residual(b - 1)

            batches(dve, first, step, chain, 2 * 2)
            normalise(NB - 1)
            low_a(NB - 1)
            residual(NB - 1)

        @block.tensor
        def _(pe):
            pe.sem_inc(pv_done, HKV)
            pe.wait_ge(w_low, 2)
            pe.wait_ge(zeroed, 6)
            pe.wait_ge(loaded, 16 * NLOAD)

            def project(b, par):
                pe.wait_ge(x_h, b + 1)
                pe.wait_ge(x_l, b + 1)
                if not early(b):
                    pe.wait_ge(qkv_used, b)
                for c in range(KC):
                    pe.matmul(bank_qkv[:, 0:QKV], xh[par][:, c, :], w_qkv_h[:, c, :], start=(c == 0), stop=False)
                    pe.matmul(bank_qkv[:, 0:QKV], xh[par][:, c, :], w_qkv_l[:, c, :], start=False, stop=False)
                    mm = pe.matmul(bank_qkv[:, 0:QKV], xl[par][:, c, :], w_qkv_h[:, c, :], start=False, stop=(c == KC - 1))
                mm.then_inc(qkv_ready, 1)

            def turn_stack(b, r):
                if r == 0:
                    pe.wait_ge(stacked, b + 1)
                if not (early(b) and r == 0):
                    pe.wait_ge(stackT_used, 3 * b + r)
                for j in range(G if r < 2 else 2):
                    src = q_stack[:, r * G + j] if r < 2 else k_stack[:, j]
                    mm = pe.transpose(bank_stack[0:STACK, j * P:(j + 1) * P],
                                      src.rearrange("p a c -> p (a c)").bitcast(F32), ident[:])
                mm.then_inc(stackT_ready, 1)

            def scores(b, par, n):
                if n == 0:
                    pe.wait_ge(stackT_used, 3 * b + 3)
                if not (early(b) and n < 2):
                    pe.wait_ge(p_ready, 8 * b + n - 1)
                h, j = n // G, n % G
                pe.matmul(bank_s[n % 2][:], qT[par][:, h * G + j, :],
                          kbd[par][:, h].rearrange("p g k -> p (g k)"), start=True, stop=True).then_inc(s_ready, 1)

            def turn_p(b, n):
                pe.wait_ge(p_ready, 8 * b + n + 1)
                if not (early(b) and n < 2):
                    pe.wait_ge(pT_low, 8 * b + n - 1)
                for g in range(HALF):
                    mm = pe.transpose(bank_p[n % 2][:, g * P:(g + 1) * P], probs[n % 4][:, g, :], ident[:])
                mm.then_inc(pT_ready, 1)

            def weigh(b, par, kv):
                h = 2 * par + kv // HALF
                if kv % HALF == 0:
                    pe.wait_ge(pT_low, 8 * b + G * (kv // HALF + 1))
                if kv == 0:
                    pe.wait_ge(v_ready, b + 1)
                    if not early(b):
                        pe.wait_ge(oT_kept, b)
                ph = pT_h[h][:, kv % HALF].rearrange("p j t -> p (j t)")
                pl = pT_l[h][:, kv % HALF].rearrange("p j t -> p (j t)")
                wh, wl = (v[par][:, kv * PVW:(kv + 1) * PVW] for v in (v_h, v_l))
                pe.matmul(bank_o[0:PVW, :], wh, ph, start=(kv == 0), stop=False)
                pe.matmul(bank_o[0:PVW, :], wh, pl, start=False, stop=False)
                pe.matmul(bank_o[0:PVW, :], wl, ph, start=False, stop=(kv == HKV - 1)).then_inc(pv_done, 1)

            def turn_o(b):
                pe.wait_ge(oT_kept, b + 1)
                pe.wait_ge(y_used, b + 1)
                for j in range(G):
                    mm = pe.transpose(bank_y[:, j * PVW:(j + 1) * PVW], oT[:, j, :], ident[0:PVW, 0:PVW])
                mm.then_inc(o_ready, 1)

            def turn_attn(b):
                pe.wait_ge(attn_ready, b + 1)
                flat = attn[:].rearrange("p g j d -> p (g j d)")
                for c in range(KC):
                    mm = pe.transpose(bank_y[:, c * P:(c + 1) * P], flat[:, c * P:(c + 1) * P], ident[:])
                mm.then_inc(aT_ready, 1)

            def out_product(b):
                pe.wait_ge(aT_low, b + 1)
                for c in range(KC):
                    pe.matmul(bank_y[:, 0:D], aT_h[:, c, :], w_o_h[:, c, :], start=(c == 0), stop=False)
                    pe.matmul(bank_y[:, 0:D], aT_h[:, c, :], w_o_l[:, c, :], start=False, stop=False)
                    mm = pe.matmul(bank_y[:, 0:D], aT_l[:, c, :], w_o_h[:, c, :], start=False, stop=(c == KC - 1))
                mm.then_inc(y_ready, 1)

            def first():
                project(0, 0)
                project(1, 1)
                for r in range(3):
                    turn_stack(0, r)
                for n in range(3):
                    scores(0, 0, n)

            def step(b, par, tail, front):
                for n in range(8):
                    turn_p(b, n)
                    if tail:
                        for kv in WEIGH_NEXT.get(n, ()):
                            weigh(b - 1, 1 - par, kv)
                    for kv in WEIGH_SAME.get(n, ()):
                        weigh(b, par, kv)
                    if n in (0, 2, 4) and front:
                        turn_stack(b + 1, n // 2)
                    if n == 2 and front:
                        project(b + 2, par)
                    if n == 3 and tail:
                        turn_o(b - 1)
                    if n == 5 and tail:
                        turn_attn(b - 1)
                    if n == 7 and tail:
                        out_product(b - 1)
                    if n < 5:
                        scores(b, par, n + 3)
                    elif front:
                        scores(b + 1, 1 - par, n - 5)

            batches(pe, first, step)
            for kvs in WEIGH_NEXT.values():
                for kv in kvs:
                    weigh(NB - 1, 1, kv)
            turn_o(NB - 1)
            turn_attn(NB - 1)
            out_product(NB - 1)



XG, XH, XD = 8, 2, 128
PAIRS = XG // 2
PH = 2 * XH
KINDS = 4
FP8_MAX = 448.0
COLS = dict(q=0, qx=PH * XD, kx=2 * PH * XD, vx=2 * PH * XD + 2 * XD, k=3 * PH * XD, v=3 * PH * XD + 2 * XD)
WCOLS = 4 * PH * XD


def steps_of_fp8(dve, link, y, magic, done=None):
    link(dve.tensor_scalar(y, y, FP8_MAX, -FP8_MAX, ALU.min, ALU.max))
    link(dve.tensor_scalar(magic.bitcast(U16), y.bitcast(U16), 0x7F80, 0x0040, ALU.bitwise_and, ALU.bitwise_or))
    last = dve.tensor_scalar(magic, magic, 1.5 * 2.0 ** -6, 2.0 ** 20, ALU.max, ALU.mult)
    if done:
        last.then_inc(done, 1)
    else:
        link(last)


class LoadsOfB:

    def __init__(self, nc, a, sem, ctx):
        def sb(name, shape, dt):
            return ctx.enter_context(nc.sbuf_tensor("sb_" + name, shape, dt))

        self.a = a
        self.ctxT = sb("ctxT", [P, KC, NT], F32)
        self.w_raw = sb("w_raw", [P, KC, WCOLS], F32)
        self.wp_raw = sb("wp_raw", [P, 2 * PH, D], F32)
        self.in_scale, self.w_scale = sb("b_in_scale", [P, KINDS, KC], F32), sb("w_scale", [P, KINDS], F32)
        self.smooth = sb("smooth", [P, 2, XG * XH], F32)
        self.norm_w, self.norm_b = sb("norm_w", [P, 4], F32), sb("norm_b", [P, 4], F32)
        self.out_scale = sb("out_scale", [P, 2], F32)
        self.loaded, self.ctx_loaded, self.w_loaded = sem("b_loaded"), sem("ctx_loaded"), sem("w_loaded")

    def start(self, sp):
        a = self.a
        self.load_pair(sp, 0)
        for dst, src in (
            (self.in_scale, a["in_scale"]),
            (self.w_scale, a["w_scale"].to_broadcast([P, KINDS])),
            (self.smooth, a["smooth"]),
            (self.norm_w, a["norm_w"]),
            (self.norm_b, a["norm_b"]),
            (self.out_scale, a["out_scale"].to_broadcast([P, 2])),
        ):
            sp.dma_start(dst[:], src).then_inc(self.loaded, 16)
        sp.dma_start(self.ctxT[:], a["ctxT"].rearrange("(c p) t -> p c t", p=P)).then_inc(self.ctx_loaded, 16)

    def load_pair(self, sp, gp):
        a = self.a
        sp.dma_start(self.w_raw[:], a["w_pairs"][bass.ds(gp, 1)].rearrange("a (c p) n -> p (a c) n", p=P)).then_inc(self.w_loaded, 16)
        sp.dma_start(self.wp_raw[:], a["wproj_pairs"][bass.ds(gp, 1)].rearrange("a k p n -> p (a k) n")).then_inc(self.w_loaded, 16)


def stage_l(nc, a, sem, banks, xres, small, ident, xq, ahead):
    inner = ExitStack()

    def sb(name, shape, dt):
        return inner.enter_context(nc.sbuf_tensor("sb_" + name, shape, dt))

    stats, mean, var, half, tmp, rstd, bits = (small[n] for n in ("stats", "mean", "var", "half", "tmp", "rstd", "bits"))
    z = [sb(f"z{i}", [P, D], F32) for i in range(2)]
    lnT = sb("lnT", [P, KC, NT], F32)
    ln_wb = sb("ln_wb", [P, 2, KC], F32)
    in_scale, in_recip = sb("in_scale", [P, KINDS, KC], F32), sb("in_recip", [P, KINDS, KC], F32)
    y = [sb(f"yq{i}", [P, NT], BF16) for i in range(2)]
    magic = [sb(f"magic{i}", [P, NT], BF16) for i in range(2)]
    total = [sb(f"total{i}", [P, NT], F32) for i in range(2)]

    loaded = sem("l_loaded")
    z_ready, zT_ready, zT_kept = sem("z_ready"), sem("zT_ready"), sem("zT_kept")
    recip_ready, y_scaled, total_ready, y_rounded = (sem(n) for n in ("recip_ready", "y_scaled", "total_ready", "y_rounded"))
    magic_ready = sem("magic_ready")
    l_dve = sem("l_dve")
    steps = [(kind, c) for kind in range(KINDS) for c in range(KC)]

    with inner, nc.Block() as block:

        @block.sync
        def _(sp):
            sp.dma_start(ln_wb[:], a["ln_wb"]).then_inc(loaded, 16)
            sp.dma_start(in_scale[:], a["in_scale"]).then_inc(loaded, 16)
            ahead.start(sp)

        @block.vector
        def _(dve):
            chain = Chain(dve, l_dve)
            link = chain.link
            dve.wait_ge(loaded, 32)
            dve.reciprocal(in_recip[:], in_scale[:]).then_inc(recip_ready, 1)
            mean_var_steps(dve, link, stats, mean[:], var[:], tmp[:])
            rsqrt_steps(dve, link, var[:], half[:], bits[:], tmp[:], rstd[:])
            with dve.Fori(0, NB // TURNS) as i:
                chain.enter(i, 2)
                rows = [bass.ds(TURNS * i + k, 1) for k in range(TURNS)]
                for b in rows:
                    r = xres[:, b, :].rearrange("p b d -> p (b d)")
                    ins = dve.tensor_scalar(r, r, mean[:, b], rstd[:, b], ALU.subtract, ALU.mult)
                link(ins)
                for b in rows:
                    ins = dve.bn_stats(stats[:, b, :].rearrange("p b s -> p (b s)"), xres[:, b, :].rearrange("p b d -> p (b d)"))
                link(ins)
                chain.leave(NB // TURNS)
            mean_var_steps(dve, link, stats, mean[:], var[:], tmp[:])
            rsqrt_steps(dve, link, var[:], half[:], bits[:], tmp[:], rstd[:])
            dve.sem_inc(zT_ready, 2)
            with dve.Fori(0, NB // 2) as i:
                for k in range(2):
                    b = 2 * i + k
                    r = xres[:, bass.ds(b, 1), :].rearrange("p b d -> p (b d)")
                    dve.wait_ge(zT_ready, b + 1)
                    dve.tensor_scalar(z[k][:], r, mean[:, bass.ds(b, 1)], rstd[:, bass.ds(b, 1)],
                                      ALU.subtract, ALU.mult).then_inc(z_ready, 1)

            def round_down(n):
                kind, c = steps[n]
                dve.wait_ge(total_ready, n + 1)
                dve.tensor_tensor(xq[:, kind, c, 0:NT], total[n % 2][:], magic[n % 2][:], ALU.subtract).then_inc(y_rounded, 1)

            for n in range(len(steps)):
                dve.wait_ge(y_scaled, n + 1)
                if n >= 2:
                    dve.wait_ge(y_rounded, n - 1)
                steps_of_fp8(dve, link, y[n % 2][:], magic[n % 2][:], magic_ready)
                if n >= 1:
                    round_down(n - 1)
            round_down(len(steps) - 1)

        @block.gpsimd
        def _(pool):
            for n in range(len(steps)):
                pool.wait_ge(magic_ready, n + 1)
                pool.tensor_tensor(total[n % 2][:], y[n % 2][:], magic[n % 2][:], ALU.add).then_inc(total_ready, 1)

        @block.tensor
        def _(pe):
            pe.sem_inc(zT_kept, 2)
            with pe.Fori(0, NB // 2) as i:
                for k in range(2):
                    b = 2 * i + k
                    pe.wait_ge(zT_kept, b + 1)
                    pe.wait_ge(z_ready, b + 1)
                    for c in range(KC):
                        mm = pe.transpose(banks[k][:, c * P:(c + 1) * P], z[k][:, c * P:(c + 1) * P], ident[:])
                    mm.then_inc(zT_ready, 1)

        @block.scalar
        def _(act):
            with act.Fori(0, NB // 2) as i:
                for k in range(2):
                    b = 2 * i + k
                    for c in range(KC):
                        if c == 0:
                            act.wait_ge(zT_ready, b + 3)
                        act.wait_ge(loaded, 32)
                        ins = act.activation(lnT[:, c, bass.ds(b * T, T)], banks[k][:, c * P:(c + 1) * P], ACT.Identity,
                                             bias=ln_wb[:, 1, c:c + 1], scale=ln_wb[:, 0, c:c + 1])
                    ins.then_inc(zT_kept, 1)
            act.wait_ge(zT_kept, NB + 2)
            act.wait_ge(recip_ready, 1)
            for n, (kind, c) in enumerate(steps):
                if n >= 2:
                    act.wait_ge(y_rounded, n - 1)
                act.activation(y[n % 2][:], lnT[:, c, :], ACT.Identity, scale=in_recip[:, kind, c:c + 1]).then_inc(y_scaled, 1)


def stage_b(nc, a, sem, banks, xres, ident, xq, ahead):
    inner = ExitStack()

    def sb(name, shape, dt):
        return inner.enter_context(nc.sbuf_tensor("sb_" + name, shape, dt))

    def pair(name, shape, dt):
        return [sb(f"{name}{i}", shape, dt) for i in range(2)]

    bank_f = banks[0:4]
    bank_t = banks[4:6]
    bank_s = banks[6:8]

    ctxT, w_raw, wp_raw, in_scale, w_scale, smooth, norm_w, norm_b, out_scale = (
        ahead.ctxT, ahead.w_raw, ahead.wp_raw, ahead.in_scale, ahead.w_scale, ahead.smooth,
        ahead.norm_w, ahead.norm_b, ahead.out_scale)
    loaded, ctx_loaded, w_loaded = ahead.loaded, ahead.ctx_loaded, ahead.w_loaded
    w_h, w_l = sb("w_h", [P, KC, WCOLS], F32R), sb("w_l", [P, KC, WCOLS], F32R)
    wmean = sb("wmean", [P, KC, 3 * PH], F32)
    wp = sb("wp", [P, 2 * PH, D], BF16)
    fold = sb("fold", [P, KINDS, KC], F32)
    smooth_r = sb("smooth_r", [P, 2, XG * XH], F32)
    xs = pair("xs", [P, KINDS, KC, P], F32R)
    c_h, c_l = sb("c_h", [P, KC, P], F32R), sb("c_l", [P, KC, P], F32R)
    square = sb("square", [P, 3 * PH, XD], BF16)
    sumsq = sb("sumsq", [P, 3 * PH], F32)
    nvar, nrstd, minus_half = (sb(n, [P, 3 * PH], F32) for n in ("nvar", "nrstd", "minus_half"))
    normed = sb("normed", [P, 3, PH, XD], F32)
    qT, qxT, kT = sb("qTb", [P, PH, P], F32), sb("qxT", [P, PH, P], F32), sb("kTb", [P, PH, P], F32)
    vv = pair("vv", [P, PH, XD], F32)
    negmax = sb("negmax", [P, 2, PH], F32)
    psum_, precip = sb("psum_", [P, 2, PH], F32), sb("precip", [P, 2, PH], F32)
    probs = sb("b_probs", [P, 2, PH, P], F32)
    pT = sb("b_pT", [P, 2, PH, P], F32)
    yb, magic = sb("yb", [P, 2, PH, P], BF16), sb("magic_b", [P, 2, PH, P], BF16)
    total = sb("total_b", [P, 2, PH, P], F32)
    catq = sb("catq", [P, 2, PH, P], BF16)

    w_folded = sem("w_folded")
    w_centred, w_high, w_ready = sem("w_centred"), sem("w_high"), sem("w_ready")
    set_up, norm_scaled = sem("b_set_up"), sem("norm_scaled")
    pool_turn, c_split, c_ready = sem("pool_turn"), sem("c_split"), sem("ctx_ready")
    xs_ready, f_ready = sem("xs_ready"), sem("f_ready")
    var_ready, rstd_ready = sem("var_ready"), sem("rstd_ready")
    ss_ready, normed_ready = sem("ss_ready"), sem("normed_ready")
    x_ready, x_kept = sem("xT_ready"), sem("xT_kept")
    s_ready, max_ready, exp_done = sem("bs_ready"), sem("max_ready"), sem("exp_done")
    p_ready, pT_ready, pT_kept = sem("bp_ready"), sem("bpT_ready"), sem("bpT_kept")
    o_ready, o_used = sem("bo_ready"), sem("bo_used")
    magic_ready, total_ready, cat_ready = sem("b_magic_ready"), sem("b_total_ready"), sem("cat_ready")
    y_ready, y_used = sem("by_ready"), sem("by_used")
    b_dve = sem("b_dve")
    PROJ = [("q", None, 0), ("qx", None, 1), ("kx", "vx", None), ("k", "v", 2)]
    SCALE = float(XD) ** -0.5
    TURN = {"k": 0, 0: 1, "out": 0, 1: 1, "q": 0, "qx": 1}
    CONVERTS = NB + 1

    def units(eng, before, first, step, end, chain=None, per_pair=0, per_round=0):
        with eng.Fori(0, PAIRS) as gp:
            if chain:
                chain.enter(gp, per_pair)
            U0 = gp * NB
            before(gp)
            first(gp, U0)
            step(U0, gp, 0, False, True)
            with eng.Fori(0, (NB - 2) // 2) as i:
                if chain:
                    chain.enter(i, per_round)
                for k in (1, 2):
                    step(U0 + 2 * i + k, gp, 2 * i + k, True, True, k % 2)
                if chain:
                    chain.leave((NB - 2) // 2)
            step(U0 + NB - 1, gp, NB - 1, True, False, 1)
            end(U0 + NB - 1, NB - 1, gp)
            if chain:
                chain.leave(PAIRS)

    with inner, nc.Block() as block:

        @block.sync
        def _(sp):
            with sp.Fori(1, PAIRS) as gp:
                sp.wait_ge(w_ready, 3 * gp)
                ahead.load_pair(sp, gp)

        @block.gpsimd
        def _(pool):
            def split_context(V, b):
                pool.wait_ge(f_ready, 4 * V + 3)
                pool.sem_inc(pool_turn, 1)
                pool.tensor_copy(c_h[:], ctxT[:, :, bass.ds(b * T, T)]).then_inc(c_split, 1)
                pool.wait_ge(c_split, V + 1)
                pool.sem_inc(pool_turn, 1)
                pool.tensor_tensor(c_l[:], ctxT[:, :, bass.ds(b * T, T)], c_h[:].bitcast(F32),
                                   ALU.subtract).then_inc(c_ready, 1)

            def deviations(V, n):
                cols = slice(0, 2 * PH) if n == 0 else slice(2 * PH, 3 * PH)
                pool.wait_ge(ss_ready, 2 * V + n + 1)
                pool.sem_inc(pool_turn, 1)
                pool.tensor_scalar(nvar[:, cols], sumsq[:, cols], EPS, None, ALU.add).then_inc(var_ready, 1)
                pool.wait_ge(var_ready, 2 * V + n + 1)
                pool.sem_inc(pool_turn, 1)
                pool.tensor_tensor(nrstd[:, cols], nvar[:, cols], minus_half[:, cols], ALU.pow).then_inc(rstd_ready, 1)

            pool.memset(minus_half[:], -0.5).then_inc(set_up, 1)
            pool.memset(xq[:, :, :, NT:NT + T], 0.0).then_inc(set_up, 1)
            pool.wait_ge(set_up, 2)
            pool.wait_ge(ctx_loaded, 16)

            def first(gp, U0):
                split_context(U0, 0)
                deviations(U0, 0)
                deviations(U0, 1)

            def round_add(U):
                pool.wait_ge(magic_ready, U + 1)
                pool.sem_inc(pool_turn, 1)
                pool.tensor_tensor(total[:], yb[:], magic[:], ALU.add).then_inc(total_ready, 1)

            def step(U, gp, b, tail, front, par=0):
                if front:
                    split_context(U + 1, b + 1)
                if tail:
                    round_add(U - 1)
                if front:
                    deviations(U + 1, 0)
                    deviations(U + 1, 1)

            def before(gp):
                pool.wait_ge(w_high, 2 * gp + 1)
                pool.sem_inc(pool_turn, 1)
                pool.tensor_tensor(w_l[:, 0], w_raw[:, 0], w_h[:, 0].bitcast(F32), ALU.subtract).then_inc(w_ready, 1)

            units(pool, before, first, step, lambda U, b, gp: round_add(U))

        @block.scalar
        def _(act):
            act.wait_ge(loaded, 16 * 6)
            act.wait_ge(set_up, 2)
            act.wait_ge(norm_scaled, 2)

            def before(gp):
                act.wait_ge(w_loaded, 32 * gp + 32)
                for n, name in enumerate(("q", "qx", "k", "v")):
                    w = w_raw[:, 1, COLS[name]:COLS[name] + (PH if n < 2 else 2) * XD]
                    ins = act.activation(w, w, ACT.Copy, scale=fold[:, n, 1:2])
                ins.then_inc(w_folded, 1)
                act.wait_ge(w_centred, 2 * gp + 1)
                act.activation(w_h[:, 0], w_raw[:, 0], ACT.Copy).then_inc(w_high, 1)
                act.wait_ge(w_centred, 2 * gp + 2)
                act.activation(w_h[:, 1], w_raw[:, 1], ACT.Copy).then_inc(w_high, 1)
                act.activation(wp[:], wp_raw[:], ACT.Copy).then_inc(w_ready, 1)

            def squares(U, par, r):
                act.wait_ge(f_ready, 4 * U + r + 5)
                col = (0, PH, 2 * PH, 2 * PH + 2)[r]
                for h in range(PH if r < 2 else 2):
                    ins = act.activation(square[:, col + h, :], bank_f[r][:, h * XD:(h + 1) * XD], ACT.Square,
                                         scale=float(XD) ** -0.5, accum_out=sumsq[:, col + h:col + h + 1])
                if r >= 2:
                    ins = act.activation(vv[par][:, 2 * (r - 2):2 * (r - 2) + 2, :].rearrange("p g d -> p (g d)"),
                                         bank_f[r][:, 2 * XD:4 * XD], ACT.Copy)
                if r % 2 == 1:
                    ins.then_inc(ss_ready, 1)

            def keep(U, r):
                act.wait_ge(x_ready, 3 * U + r + 1)
                bank = bank_t[TURN[("q", "qx", "k")[r]]]
                if r < 2:
                    ins = act.activation((qT, qxT)[r][:].rearrange("p h t -> p (h t)"), bank[:], ACT.Identity,
                                         bias=norm_b[:, r:r + 1], scale=norm_w[:, r:r + 1])
                else:
                    for k in range(2):
                        ins = act.activation(kT[:, 2 * k:2 * k + 2, :].rearrange("p h t -> p (h t)"),
                                             bank[:, 2 * k * P:2 * (k + 1) * P], ACT.Identity,
                                             bias=norm_b[:, 2 + k:3 + k], scale=norm_w[:, 2 + k:3 + k])
                ins.then_inc(x_kept, 1)

            def exps(U, s):
                act.wait_ge(max_ready, 2 * U + s + 1)
                for h in range(PH):
                    ins = act.activation(probs[:, s, h, :], bank_s[s][:, h * P:(h + 1) * P], ACT.Exp,
                                         bias=negmax[:, s, h:h + 1], accum_out=psum_[:, s, h:h + 1])
                ins.then_inc(exp_done, 1)

            def keep_p(U, s):
                act.wait_ge(pT_ready, 2 * U + s + 1)
                act.activation(pT[:, s].rearrange("p h t -> p (h t)"), bank_t[TURN[s]][:], ACT.Copy).then_inc(pT_kept, 1)

            def first(gp, U0):
                for r in range(4):
                    squares(U0, 0, r)
                keep(U0, 0)
                keep(U0, 1)

            def step(U, gp, b, tail, front, par=0):
                nxt = 1 - par
                keep(U, 2)
                if front:
                    squares(U + 1, nxt, 0)
                    squares(U + 1, nxt, 1)
                exps(U, 0)
                exps(U, 1)
                keep_p(U, 0)
                if front:
                    squares(U + 1, nxt, 2)
                    squares(U + 1, nxt, 3)
                keep_p(U, 1)
                if front:
                    keep(U + 1, 0)
                    keep(U + 1, 1)

            units(act, before, first, step, lambda U, b, gp: None)

        @block.vector
        def _(dve):
            chain = Chain(dve, b_dve)
            link = chain.link
            dve.wait_ge(loaded, 16 * 6)
            link(dve.reciprocal(smooth_r[:], smooth[:]))
            link(dve.tensor_tensor(fold[:], in_scale[:], ap_bcast(w_scale[:], 2, KC), ALU.mult))
            link(dve.tensor_tensor(out_scale[:, 0:1], out_scale[:, 0:1], out_scale[:, 1:2], ALU.mult))
            for t in (norm_w, norm_b):
                dve.tensor_scalar(t[:, 0:2], t[:, 0:2], SCALE, None, ALU.mult).then_inc(norm_scaled, 1)
            dve.sem_inc(normed_ready, 4)
            dve.sem_inc(o_used, 2)
            dve.sem_inc(y_used, 2)

            def before(gp):
                for b in range(2):
                    convert(CONVERTS * gp + b, b, b, 4 * NB * gp + 4)
                dve.wait_ge(w_loaded, 32 * gp + 32)
                for n, name in enumerate(("q", "qx", "k", "v")):
                    w = w_raw[:, 0, COLS[name]:COLS[name] + (PH if n < 2 else 2) * XD]
                    ins = dve.tensor_scalar(w, w, fold[:, n, 0:1], None, ALU.mult)
                link(ins)
                for c in range(KC):
                    if c == 1:
                        dve.wait_ge(w_folded, gp + 1)
                    qs = w_raw[:, c, 0:2 * PH * XD].rearrange("p (h d) -> p h d", d=XD)
                    ks = w_raw[:, c, 2 * PH * XD:WCOLS].rearrange("p (s h d) -> p s h d", s=2, d=XD)[:, :, 0:2, :]
                    mq = wmean[:, c, 0:2 * PH]
                    mk = wmean[:, c, 2 * PH:3 * PH].rearrange("p (s h) -> p s h", s=2)
                    dve.tensor_reduce(mq, qs, AX_X, ALU.add)
                    link(dve.tensor_reduce(mk, ks, AX_X, ALU.add))
                    link(dve.tensor_scalar(wmean[:, c], wmean[:, c], 1.0 / XD, None, ALU.mult))
                    dve.tensor_tensor(qs, qs, ap_bcast(mq, 2, XD), ALU.subtract)
                    for s in range(2):
                        ins = dve.tensor_tensor(ks[:, s], ks[:, s], ap_bcast(mk[:, s], 2, XD), ALU.subtract)
                    ins.then_inc(w_centred, 1)
                dve.wait_ge(w_high, 2 * gp + 2)
                dve.tensor_tensor(w_l[:, 1], w_raw[:, 1], w_h[:, 1].bitcast(F32), ALU.subtract).then_inc(w_ready, 1)

            def convert(n, b, par, used):
                dve.wait_ge(f_ready, used)
                dve.tensor_copy(xs[par][:].rearrange("p k c t -> p (k c) t"),
                                xq[:, :, :, bass.ds(b * T, T)].rearrange("p k c t -> p (k c) t")).then_inc(xs_ready, 1)

            def norms(U, n):
                dve.wait_ge(rstd_ready, 2 * U + n + 1)
                for r in range(2):
                    if n == 0:
                        dve.tensor_tensor(normed[:, r], bank_f[r][:].rearrange("p (h d) -> p h d", h=PH),
                                          ap_bcast(nrstd[:, r * PH:(r + 1) * PH], 2, XD), ALU.mult).then_inc(normed_ready, 1)
                    else:
                        dve.tensor_tensor(normed[:, 2, 2 * r:2 * r + 2], bank_f[2 + r][:, 0:2 * XD].rearrange("p (h d) -> p h d", h=2),
                                          ap_bcast(nrstd[:, 2 * PH + 2 * r:2 * PH + 2 * r + 2], 2, XD),
                                          ALU.mult).then_inc(normed_ready, 1)

            def maxima(U, s):
                dve.wait_ge(s_ready, 2 * U + s + 1)
                dve.tensor_reduce(negmax[:, s], bank_s[s][:].rearrange("p (h k) -> p h k", h=PH), AX_X, ALU.max,
                                  negate=True).then_inc(max_ready, 1)

            def weights(U, s):
                dve.wait_ge(exp_done, 2 * U + s + 1)
                link(dve.reciprocal(precip[:, s], psum_[:, s]))
                dve.tensor_tensor(probs[:, s], probs[:, s], ap_bcast(precip[:, s], 2, P), ALU.mult).then_inc(p_ready, 1)

            def scaled(U, s, gp):
                dve.wait_ge(o_ready, 2 * U + s + 1)
                ins = dve.tensor_tensor(yb[:, s], bank_s[s][:].rearrange("p (h t) -> p h t", h=PH),
                                        ap_bcast(smooth_r[:, s, bass.ds(gp * PH, PH)], 2, P), ALU.mult)
                ins.then_inc(o_used, 1)

            def round_up(U):
                dve.wait_ge(o_used, 2 * U + 4)
                steps_of_fp8(dve, link, yb[:], magic[:], magic_ready)

            def round_down(U):
                dve.wait_ge(total_ready, U + 1)
                dve.tensor_tensor(catq[:], total[:], magic[:], ALU.subtract).then_inc(cat_ready, 1)

            def add_out(U, b):
                dve.wait_ge(y_ready, U + 1)
                r = xres[:, bass.ds(b, 1), :]
                dve.scalar_tensor_tensor(out=r, in0=bank_t[TURN["out"]][:, 0:D].unsqueeze(1), scalar=out_scale[:, 0:1],
                                         in1=r, op0=ALU.mult, op1=ALU.add).then_inc(y_used, 1)

            def first(gp, U0):
                norms(U0, 0)
                norms(U0, 1)

            def step(U, gp, b, tail, front, par=0):
                if tail:
                    scaled(U - 1, 0, gp)
                    scaled(U - 1, 1, gp)
                    round_up(U - 1)
                if front:
                    convert(CONVERTS * gp + b + 2, b + 2, par, 4 * U + 8)
                maxima(U, 0)
                maxima(U, 1)
                if tail:
                    round_down(U - 1)
                weights(U, 0)
                weights(U, 1)
                if front:
                    norms(U + 1, 0)
                if tail:
                    add_out(U - 1, b - 1)
                if front:
                    norms(U + 1, 1)

            def last(U, b, gp):
                scaled(U, 0, gp)
                scaled(U, 1, gp)
                round_up(U)
                round_down(U)
                add_out(U, b)

            step_links = 2 + 2
            units(dve, before, first, step, last, chain,
                  1 + KC * 2 + NB * step_links, 2 * step_links)

        @block.tensor
        def _(pe):
            def project(U, gp, b, par, r):
                if r == 0:
                    pe.wait_ge(xs_ready, CONVERTS * gp + b + 1)
                if r == 2:
                    pe.wait_ge(c_ready, U + 1)
                pe.wait_ge(normed_ready, 4 * U + r + 1)
                bank = bank_f[r]
                left, right, kind = PROJ[r]
                if r < 2:
                    cols = slice(COLS[left], COLS[left] + PH * XD)
                    for c in range(KC):
                        pe.matmul(bank[:], xs[par][:, kind, c, :], w_h[:, c, cols], start=(c == 0), stop=False)
                        mm = pe.matmul(bank[:], xs[par][:, kind, c, :], w_l[:, c, cols], start=False, stop=(c == KC - 1))
                elif r == 2:
                    cols = slice(COLS["kx"], COLS["kx"] + 4 * XD)
                    for c in range(KC):
                        pe.matmul(bank[:], c_h[:, c, :], w_h[:, c, cols], start=(c == 0), stop=False)
                        pe.matmul(bank[:], c_h[:, c, :], w_l[:, c, cols], start=False, stop=False)
                        mm = pe.matmul(bank[:], c_l[:, c, :], w_h[:, c, cols], start=False, stop=(c == KC - 1))
                else:
                    for n, name in enumerate(("k", "v")):
                        cols = slice(COLS[name], COLS[name] + 2 * XD)
                        out = bank[:, n * 2 * XD:(n + 1) * 2 * XD]
                        for c in range(KC):
                            pe.matmul(out, xs[par][:, 2 + n, c, :], w_h[:, c, cols], start=(c == 0), stop=False)
                            mm = pe.matmul(out, xs[par][:, 2 + n, c, :], w_l[:, c, cols], start=False, stop=(c == KC - 1))
                mm.then_inc(f_ready, 1)

            def turn(U, r):
                pe.wait_ge(normed_ready, 4 * U + (r + 5 if r < 2 else 8))
                for h in range(PH):
                    mm = pe.transpose(bank_t[TURN[("q", "qx", "k")[r]]][:, h * P:(h + 1) * P], normed[:, r, h, :], ident[:])
                mm.then_inc(x_ready, 1)

            def scores(U, s):
                q, kcol = (qT, 2) if s == 0 else (qxT, 0)
                pe.wait_ge(x_kept, 3 * U + 3)
                pe.wait_ge(o_used, 2 * U + s + 1)
                for h in range(PH):
                    mm = pe.matmul(bank_s[s][:, h * P:(h + 1) * P], q[:, h, :], kT[:, kcol + h // XH, :], start=True, stop=True)
                mm.then_inc(s_ready, 1)

            def turn_p(U, s):
                pe.wait_ge(p_ready, 2 * U + s + 1)
                for h in range(PH):
                    mm = pe.transpose(bank_t[TURN[s]][:, h * P:(h + 1) * P], probs[:, s, h, :], ident[:])
                mm.then_inc(pT_ready, 1)

            def weigh(U, par, s):
                pe.wait_ge(pT_kept, 2 * U + s + 1)
                vcol = 2 if s == 0 else 0
                for g in range(2):
                    mm = pe.matmul(bank_s[s][:, g * XH * P:(g + 1) * XH * P], vv[par][:, vcol + g, :],
                                   pT[:, s, g * XH:(g + 1) * XH, :].rearrange("p h t -> p (h t)"), start=True, stop=True)
                mm.then_inc(o_ready, 1)

            def out_product(U):
                pe.wait_ge(cat_ready, U + 1)
                for n in range(2 * PH):
                    mm = pe.matmul(bank_t[TURN["out"]][:, 0:D], catq[:, n // PH, n % PH, :], wp[:, n, :],
                                   start=(n == 0), stop=(n == 2 * PH - 1))
                mm.then_inc(y_ready, 1)

            pe.sem_inc(f_ready, 4)

            def before(gp):
                pe.wait_ge(w_ready, 3 * gp + 3)

            def first(gp, U0):
                for r in range(4):
                    project(U0, gp, 0, 0, r)
                pe.wait_ge(y_used, U0 + 2)
                turn(U0, 0)
                turn(U0, 1)

            def step(U, gp, b, tail, front, par=0):
                nxt = 1 - par
                pe.wait_ge(x_kept, 3 * U + 2)
                turn(U, 2)
                if front:
                    project(U + 1, gp, b + 1, nxt, 0)
                    project(U + 1, gp, b + 1, nxt, 1)
                scores(U, 0)
                scores(U, 1)
                if front:
                    project(U + 1, gp, b + 1, nxt, 2)
                    project(U + 1, gp, b + 1, nxt, 3)
                turn_p(U, 0)
                if tail:
                    out_product(U - 1)
                pe.wait_ge(pT_kept, 2 * U + 1)
                turn_p(U, 1)
                weigh(U, par, 0)
                if front:
                    if tail:
                        pe.wait_ge(y_used, U + 2)
                    turn(U + 1, 0)
                    pe.wait_ge(pT_kept, 2 * U + 2)
                    turn(U + 1, 1)
                weigh(U, par, 1)

            def last(U, b, gp):
                pe.wait_ge(y_used, U + 2)
                out_product(U)

            units(pe, before, first, step, last)





NE, TOP, EH, NCH, CH = 32, 4, 96, 16, 128
E_TILES = NE * EH // P
TILES = E_TILES + NCH * CH // P
CHUNK_SCALE = 0.05
WTILE = 2 * KC * P + D
BLK = 512
SPAN = 2
PASSES = NT // (BLK * SPAN)


def stage_c(nc, a, sem, banks, xres, small, ident):
    inner = ExitStack()

    def sb(name, shape, dt):
        return inner.enter_context(nc.sbuf_tensor("sb_" + name, shape, dt))

    def pair(name, shape, dt):
        return [sb(f"{name}{i}", shape, dt) for i in range(2)]

    stats, mean, var, half, tmp, rstd, bits = (small[n] for n in ("stats", "mean", "var", "half", "tmp", "rstd", "bits"))
    x_h, x_l = sb("x2_h", [P, KC, NT], F32R), sb("x2_l", [P, KC, NT], F32R)
    cwT = sb("cwT", [P, NT], F32R)
    z = [sb(f"c_z{i}", [P, D], F32) for i in range(TURNS)]
    outT = sb("outT", [P, KC, NT], F32)
    gate, gate_h, gate_l = sb("gate", [P, KC, NE], F32), sb("gate_h", [P, KC, NE], F32R), sb("gate_l", [P, KC, NE], F32R)
    logitT = sb("logitT", [NE, NT], F32)
    names = ("logit", "prob", "key", "above", "equal", "count0", "count1")
    logit, prob, key, above, equal, count0, count1 = (sb(n, [P, NB, NE], F32) for n in names)
    top8 = sb("top8", [P, NB, 8], F32)
    rowmax, rowsum, nabove = (sb(n, [P, NB], F32) for n in ("rowmax", "rowsum", "nabove"))
    cw_high = sb("cw_high", [P, NB, 2, NE], F32R)
    cw_stack = sb("cw_stack", [P, NB, 2, 2, NE], F32)

    loaded = sem("c_loaded")
    c_dve = sem("c_dve")
    normed, turned, x_high, x_low = sem("c_normed"), sem("c_turned"), sem("c_x_high"), sem("c_x_low")
    x2_kept, c_pool_turn = sem("x2_kept"), sem("c_pool_turn")
    gate_high, gate_low = sem("gate_high"), sem("gate_low")
    logitT_ready, logitT_kept, logit_ready = sem("logitT_ready"), sem("logitT_kept"), sem("logit_ready")
    shifted, exp_ready, stack_ready = sem("c_shifted"), sem("c_exp_ready"), sem("c_stack_ready")
    cwT_ready, cwT_kept = sem("cwT_ready"), sem("cwT_kept")

    with inner:
        with nc.Block() as block:

            @block.sync
            def _(sp):
                sp.dma_start(gate[:], a["gateT"].rearrange("(c p) e -> p c e", p=P)).then_inc(loaded, 16)

            @block.scalar
            def _(act):
                act.wait_ge(loaded, 16)
                act.activation(gate_h[:], gate[:], ACT.Copy).then_inc(gate_high, 1)
                with act.Fori(0, NB // TURNS) as i:
                    for k in range(TURNS):
                        b = TURNS * i + k
                        act.wait_ge(turned, b + TURNS + 1)
                        act.activation(x_h[:, :, bass.ds(b * T, T)], banks[k][:, 0:D].rearrange("p (c t) -> p c t", c=KC),
                                       ACT.Copy).then_inc(x_high, 1)
                for n in range(NT // BLK):
                    act.wait_ge(logitT_ready, n + 1)
                    act.activation(logitT[:, n * BLK:(n + 1) * BLK], banks[2 + n][0:NE, :], ACT.Copy).then_inc(logitT_kept, 1)
                act.wait_ge(shifted, 1)
                act.activation(prob[:], prob[:], ACT.Exp).then_inc(exp_ready, 1)
                act.activation(key[:], logit[:], ACT.Exp, scale=-1.0).then_inc(exp_ready, 1)
                for n in range(NT // BLK):
                    act.wait_ge(cwT_ready, n + 1)
                    act.activation(cwT[:, n * BLK:(n + 1) * BLK], banks[2 + n][:], ACT.Copy).then_inc(cwT_kept, 1)

            @block.gpsimd
            def _(pool):
                pool.sem_inc(x2_kept, TURNS)
                with pool.Fori(0, NB // TURNS) as i:
                    for k in range(TURNS):
                        b = TURNS * i + k
                        pool.wait_ge(normed, b + 1)
                        pool.sem_inc(c_pool_turn, 1)
                        pool.tensor_copy(xres[:, bass.ds(b, 1), :].rearrange("p b d -> p (b d)"), z[k][:]).then_inc(x2_kept, 1)

            @block.vector
            def _(dve):
                chain = Chain(dve, c_dve)
                link = chain.link
                dve.sem_inc(x_low, TURNS)
                with dve.Fori(0, NB - 1) as b:
                    dve.bn_stats(stats[:, bass.ds(b, 1), :].rearrange("p b s -> p (b s)"),
                                 xres[:, bass.ds(b, 1), :].rearrange("p b d -> p (b d)"))
                link(dve.bn_stats(stats[:, NB - 1, :], xres[:, NB - 1, :]))
                mean_var_steps(dve, link, stats, mean[:], var[:], tmp[:])
                rsqrt_steps(dve, link, var[:], half[:], bits[:], tmp[:], rstd[:])
                with dve.Fori(0, NB // TURNS) as i:
                    for k in range(TURNS):
                        b = TURNS * i + k
                        r = xres[:, bass.ds(b, 1), :].rearrange("p b d -> p (b d)")
                        dve.wait_ge(turned, b + 1)
                        dve.wait_ge(x2_kept, b + 1)
                        dve.tensor_scalar(z[k][:], r, mean[:, bass.ds(b, 1)], rstd[:, bass.ds(b, 1)],
                                          ALU.subtract, ALU.mult).then_inc(normed, 1)
                    for k in range(TURNS):
                        b = TURNS * i + k
                        dve.wait_ge(x_high, b + 1)
                        dve.tensor_tensor(x_l[:, :, bass.ds(b * T, T)], banks[k][:, 0:D].rearrange("p (c t) -> p c t", c=KC),
                                          x_h[:, :, bass.ds(b * T, T)].bitcast(F32), ALU.subtract).then_inc(x_low, 1)
                dve.wait_ge(gate_high, 1)
                dve.tensor_tensor(gate_l[:], gate[:], gate_h[:].bitcast(F32), ALU.subtract).then_inc(gate_low, 1)
                dve.wait_ge(logit_ready, 1)
                link(dve.tensor_copy(logit[:], banks[0][:].rearrange("p (b e) -> p b e", b=NB)))
                link(dve.tensor_reduce(rowmax[:], logit[:], AX_X, ALU.max))
                dve.tensor_tensor(prob[:], logit[:], ap_bcast(rowmax[:], 2, NE), ALU.subtract).then_inc(shifted, 1)
                dve.wait_ge(exp_ready, 2)
                link(dve.tensor_reduce(rowsum[:], prob[:], AX_X, ALU.add))
                link(dve.reciprocal(rowsum[:], rowsum[:]))
                link(dve.tensor_tensor(prob[:], prob[:], ap_bcast(rowsum[:], 2, NE), ALU.mult))
                link(dve.tensor_scalar(key[:], key[:], 1.0, None, ALU.add))
                link(dve.reciprocal(key[:], key[:]))
                for b in range(NB):
                    ins = dve.max(top8[:, b, :], key[:, b, :])
                link(ins)
                fourth = top8[:, :, TOP - 1:TOP].to_broadcast([P, NB, NE])
                dve.tensor_tensor(above[:], key[:], fourth, ALU.is_gt)
                link(dve.tensor_tensor(equal[:], key[:], fourth, ALU.is_equal))
                link(dve.tensor_reduce(nabove[:], above[:], AX_X, ALU.add))
                src, k = equal, 1
                for n in range(NE.bit_length() - 1):
                    dst = (count0, count1)[n % 2]
                    dve.tensor_copy(dst[:, :, 0:k], src[:, :, 0:k])
                    link(dve.tensor_tensor(dst[:, :, k:NE], src[:, :, k:NE], src[:, :, 0:NE - k], ALU.add))
                    src, k = dst, 2 * k
                link(dve.tensor_tensor(src[:], src[:], ap_bcast(nabove[:], 2, NE), ALU.add))
                link(dve.scalar_tensor_tensor(out=equal[:], in0=src[:], scalar=float(TOP), in1=equal[:], op0=ALU.is_le, op1=ALU.mult))
                link(dve.tensor_tensor(above[:], above[:], equal[:], ALU.add))
                link(dve.tensor_tensor(prob[:], prob[:], above[:], ALU.mult))
                link(dve.tensor_reduce(rowsum[:], prob[:], AX_X, ALU.add))
                link(dve.reciprocal(rowsum[:], rowsum[:]))
                link(dve.tensor_tensor(prob[:], prob[:], ap_bcast(rowsum[:], 2, NE), ALU.mult))
                link(dve.tensor_scalar(key[:], prob[:], CHUNK_SCALE, None, ALU.mult))
                dve.tensor_copy(cw_high[:, :, 0, :], prob[:])
                link(dve.tensor_copy(cw_high[:, :, 1, :], key[:]))
                high = cw_high[:].bitcast(F32)
                dve.tensor_copy(cw_stack[:, :, :, 0, :], high)
                dve.tensor_tensor(cw_stack[:, :, 0, 1, :], prob[:], high[:, :, 0, :], ALU.subtract)
                dve.tensor_tensor(cw_stack[:, :, 1, 1, :], key[:], high[:, :, 1, :], ALU.subtract).then_inc(stack_ready, 1)

            @block.tensor
            def _(pe):
                pe.sem_inc(turned, TURNS)
                with pe.Fori(0, NB // TURNS) as i:
                    for k in range(TURNS):
                        b = TURNS * i + k
                        pe.wait_ge(normed, b + 1)
                        pe.wait_ge(x_low, b + 1)
                        for c in range(KC):
                            mm = pe.transpose(banks[k][:, c * P:(c + 1) * P], z[k][:, c * P:(c + 1) * P], ident[:])
                        mm.then_inc(turned, 1)
                pe.wait_ge(gate_low, 1)
                pe.wait_ge(x_low, NB + TURNS)
                for n in range(NT // BLK):
                    blk = slice(n * BLK, (n + 1) * BLK)
                    for c in range(KC):
                        out = banks[2 + n][0:NE, :]
                        pe.matmul(out, gate_h[:, c, :], x_h[:, c, blk], start=(c == 0), stop=False)
                        pe.matmul(out, gate_l[:, c, :], x_h[:, c, blk], start=False, stop=False)
                        mm = pe.matmul(out, gate_h[:, c, :], x_l[:, c, blk], start=False, stop=(c == KC - 1))
                    mm.then_inc(logitT_ready, 1)
                pe.wait_ge(logitT_kept, NT // BLK)
                for b in range(NB):
                    mm = pe.transpose(banks[0][:, b * NE:(b + 1) * NE], logitT[:, b * T:(b + 1) * T], ident[0:NE, 0:NE])
                mm.then_inc(logit_ready, 1)
                pe.wait_ge(stack_ready, 1)
                for b in range(NB):
                    mm = pe.transpose(banks[2 + b // 4][:, b % 4 * P:(b % 4 + 1) * P],
                                      cw_stack[:, b].rearrange("p s t e -> p (s t e)"), ident[:])
                    if b % 4 == 3:
                        mm.then_inc(cwT_ready, 1)

        experts(nc, a, sem, banks, x_h, x_l, cwT, outT)
        last_norm(nc, a, sem, banks, xres, small, ident, outT)


def experts(nc, a, sem, banks, x_h, x_l, cwT, outT):
    inner = ExitStack()

    def pair(name, shape, dt):
        return [inner.enter_context(nc.sbuf_tensor(f"sb_{name}{i}", shape, dt)) for i in range(2)]

    bank_out, bank_g, bank_u, bank_c = banks[0:4], banks[4], banks[5], banks[6]
    raw, w_h, w_l = pair("e_raw", [P, WTILE + P], F32), pair("e_wh", [P, WTILE + P], F32R), pair("e_wl", [P, WTILE], F32R)
    sg, act_, act_h, act_l = pair("e_sg", [P, BLK], F32), pair("e_a", [P, BLK], F32), pair("e_ah", [P, BLK], F32R), pair("e_al", [P, BLK], F32R)

    w_loaded = [sem(f"e_loaded{i}") for i in range(2)]
    w_high, w_ready, tile_done = sem("e_w_high"), sem("e_w_ready"), sem("e_tile_done")
    pool_turn = sem("e_pool_turn")
    g_ready, u_ready, c_ready = sem("g_ready"), sem("u_ready"), sem("c_ready")
    silu_ready, gated, weighted, a_high, a_low = (sem(n) for n in ("silu_ready", "gated", "weighted", "a_high", "a_low"))
    out_ready, out_kept = sem("e_out_ready"), sem("e_out_kept")
    HALFT = TILES // 2

    with inner, nc.Block() as block:

        @block.sync
        def _(sp):
            sp.sem_inc(w_ready, 2)
            with sp.Fori(0, PASSES) as th:
                with sp.Fori(0, HALFT) as i:
                    for k in range(2):
                        sp.wait_ge(w_ready, th * TILES + 2 * i + k + 1)
                        sp.dma_start(raw[k][:, 0:WTILE], a["w_tiles"][bass.ds(2 * i + k, 1)].rearrange("a p n -> (a p) n")).then_inc(w_loaded[k], 16)
                        sp.dma_start(raw[k][:, WTILE:WTILE + P], a["sel_tiles"][bass.ds(2 * i + k, 1)].rearrange("a p n -> (a p) n")).then_inc(w_loaded[k], 16)

        @block.gpsimd
        def _(pool):
            with pool.Fori(0, PASSES) as th:
                with pool.Fori(0, HALFT) as i:
                    for k in range(2):
                        pool.wait_ge(w_high, th * TILES + 2 * i + k + 1)
                        pool.sem_inc(pool_turn, 1)
                        pool.tensor_tensor(w_l[k][:], raw[k][:, 0:WTILE], w_h[k][:, 0:WTILE].bitcast(F32),
                                           ALU.subtract).then_inc(w_ready, 1)

        @block.scalar
        def _(act):
            act.activation(sg[0][:, 0:1], cwT[:, 0:1], ACT.Silu).then_inc(silu_ready, 1)
            act.sem_inc(out_kept, 1)
            act.sem_inc(tile_done, 2)
            with act.Fori(0, PASSES) as th:
                def split(t, k):
                    act.wait_ge(w_loaded[k], (th * TILES + t - k) * 16 + 32)
                    act.wait_ge(tile_done, th * TILES + t + 1)
                    act.activation(w_h[k][:], raw[k][:], ACT.Copy).then_inc(w_high, 1)

                def tile(t, k, ahead=True):
                    for s in range(SPAN):
                        q = (th * TILES + t) * SPAN + s
                        act.wait_ge(g_ready, q + 1)
                        act.activation(sg[s][:], bank_g[:], ACT.Silu).then_inc(silu_ready, 1)
                        act.wait_ge(weighted, q + 2)
                        act.activation(act_h[s][:], act_[s][:], ACT.Copy).then_inc(a_high, 1)
                        if s == 0 and ahead:
                            split(t + 1, 1 - k)

                split(0, 0)
                with act.Fori(0, HALFT - 1) as i:
                    tile(2 * i, 0)
                    tile(2 * i + 1, 1)
                tile(TILES - 2, 0)
                tile(TILES - 1, 1, ahead=False)
                act.wait_ge(out_ready, th + 1)
                for c in range(KC):
                    for s in range(SPAN):
                        ins = act.activation(outT[:, c, bass.ds(th * (SPAN * BLK) + s * BLK, BLK)], bank_out[c * SPAN + s][:], ACT.Copy)
                ins.then_inc(out_kept, 1)

        @block.vector
        def _(dve):
            dve.sem_inc(gated, 1)
            dve.sem_inc(weighted, 1)
            with dve.Fori(0, PASSES) as th:
                with dve.Fori(0, TILES) as t:
                    for s in range(SPAN):
                        q = (th * TILES + t) * SPAN + s
                        dve.wait_ge(silu_ready, q + 2)
                        dve.wait_ge(u_ready, q + 1)
                        dve.tensor_tensor(sg[s][:], sg[s][:], bank_u[:], ALU.mult).then_inc(gated, 1)
                        dve.wait_ge(gated, q + 2)
                        dve.wait_ge(c_ready, q + 1)
                        dve.tensor_tensor(act_[s][:], sg[s][:], bank_c[:], ALU.mult).then_inc(weighted, 1)
                        dve.wait_ge(a_high, q + 1)
                        dve.tensor_tensor(act_l[s][:], act_[s][:], act_h[s][:].bitcast(F32), ALU.subtract).then_inc(a_low, 1)

        @block.tensor
        def _(pe):
            def three(out, left_h, left_l, right_h, right_l, start, stop):
                pe.matmul(out, left_h, right_h, start=start, stop=False)
                pe.matmul(out, left_l, right_h, start=False, stop=False)
                return pe.matmul(out, left_h, right_l, start=False, stop=stop)

            def up(th, n, q, k, s):
                blk = bass.ds(th * (SPAN * BLK) + s * BLK, BLK)
                if s == 0:
                    pe.wait_ge(w_ready, n + 3)
                for m, (bank, ready) in enumerate(((bank_g, g_ready), (bank_u, u_ready))):
                    pe.wait_ge((silu_ready, gated)[m], q + 1)
                    for c in range(KC):
                        col = slice((m * KC + c) * P, (m * KC + c + 1) * P)
                        mm = three(bank[:], w_h[k][:, col], w_l[k][:, col], x_h[:, c, blk], x_l[:, c, blk], c == 0, c == KC - 1)
                    mm.then_inc(ready, 1)
                pe.wait_ge(weighted, q + 1)
                pe.matmul(bank_c[:], w_h[k][:, WTILE:WTILE + P], cwT[:, blk], start=True, stop=True).then_inc(c_ready, 1)

            def down(q, k, s, first, last):
                pe.wait_ge(a_low, q + 1)
                for c in range(KC):
                    col = slice(2 * KC * P + c * P, 2 * KC * P + (c + 1) * P)
                    mm = three(bank_out[c * SPAN + s][:], w_h[k][:, col], w_l[k][:, col], act_h[s][:], act_l[s][:], first, last)
                if s == SPAN - 1:
                    mm.then_inc(tile_done, 1)
                return mm

            with pe.Fori(0, PASSES) as th:
                n0, q0 = th * TILES, th * TILES * SPAN

                def tile(t, k, first=False, last=False):
                    q = q0 + t * SPAN
                    up(th, n0 + t, q + 1, k, 1)
                    down(q, k, 0, first, last)
                    if not last:
                        up(th, n0 + t + 1, q + 2, 1 - k, 0)
                    return down(q + 1, k, 1, first, last)

                up(th, n0, q0, 0, 0)
                pe.wait_ge(out_kept, th + 1)
                tile(0, 0, first=True)
                with pe.Fori(0, HALFT - 1) as i:
                    tile(2 * i + 1, 1)
                    tile(2 * i + 2, 0)
                tile(TILES - 1, 1, last=True)
                pe.wait_ge(tile_done, n0 + TILES + 2)
                pe.sem_inc(out_ready, 1)


def last_norm(nc, a, sem, banks, xres, small, ident, outT):
    stats, mean, var, half, tmp, rstd, bits = (small[n] for n in ("stats", "mean", "var", "half", "tmp", "rstd", "bits"))
    turned, added, normed, written, n_dve = (sem("n_" + n) for n in ("turned", "added", "normed", "written", "dve"))
    outT_s = sem("n_staged")

    with ExitStack() as inner, nc.Block() as block:
        stage = [inner.enter_context(nc.sbuf_tensor(f"sb_n_stage{i}", [P, KC, T], F32)) for i in range(TURNS)]

        @block.scalar
        def _(act):
            with act.Fori(0, NB // TURNS) as i:
                for k in range(TURNS):
                    b = TURNS * i + k
                    act.wait_ge(turned, b + 1)
                    act.activation(stage[k][:], outT[:, :, bass.ds(b * T, T)], ACT.Copy).then_inc(outT_s, 1)

        @block.tensor
        def _(pe):
            pe.sem_inc(turned, TURNS)
            with pe.Fori(0, NB // TURNS) as i:
                for k in range(TURNS):
                    b = TURNS * i + k
                    pe.wait_ge(outT_s, b + 1)
                    pe.wait_ge(added, b + 1)
                    for c in range(KC):
                        mm = pe.transpose(banks[k][:, c * P:(c + 1) * P], stage[k][:, c, :], ident[:])
                    mm.then_inc(turned, 1)

        @block.vector
        def _(dve):
            chain = Chain(dve, n_dve)
            link = chain.link
            dve.sem_inc(added, TURNS)
            with dve.Fori(0, NB // TURNS) as i:
                chain.enter(i, 1)
                rows = [bass.ds(TURNS * i + k, 1) for k in range(TURNS)]
                for k, b in enumerate(rows):
                    r = xres[:, b, :].rearrange("p b d -> p (b d)")
                    dve.wait_ge(turned, TURNS * i + k + TURNS + 1)
                    dve.tensor_tensor(r, r, banks[k][:, 0:D], ALU.add).then_inc(added, 1)
                dve.wait_ge(added, TURNS * i + 2 * TURNS)
                for b in rows:
                    ins = dve.bn_stats(stats[:, b, :].rearrange("p b s -> p (b s)"), xres[:, b, :].rearrange("p b d -> p (b d)"))
                link(ins)
                chain.leave(NB // TURNS)
            mean_var_steps(dve, link, stats, mean[:], var[:], tmp[:])
            rsqrt_steps(dve, link, var[:], half[:], bits[:], tmp[:], rstd[:])
            with dve.Fori(0, NB) as b:
                r = xres[:, bass.ds(b, 1), :].rearrange("p b d -> p (b d)")
                dve.tensor_scalar(r, r, mean[:, bass.ds(b, 1)], rstd[:, bass.ds(b, 1)],
                                  ALU.subtract, ALU.mult).then_inc(normed, 1)

        @block.sync
        def _(sp):
            for n in range(4):
                bs = slice(n * NB // 4, (n + 1) * NB // 4)
                sp.wait_ge(normed, (n + 1) * NB // 4)
                sp.dma_start(a["out"][bs].rearrange("b t d -> t b d"), xres[:, bs, :]).then_inc(written, 16)
            sp.wait_ge(written, 16 * 4)


def layout(inputs):
    import numpy as np

    x = np.asarray(inputs["x"])
    wq, wk, wv = (np.asarray(inputs[f"L0_attn_W{c}"]) for c in "qkv")
    bq, bk, bv = (np.asarray(inputs[f"L0_attn_b{c}"]) for c in "qkv")
    order = np.arange(D).reshape(2, HALF, G, HD).transpose(0, 2, 1, 3).reshape(D)
    out = {
        "x": x,
        "xT": x.reshape(NT, D).T,
        "w_qkvT": np.concatenate([wq[order], wk, wv]).T,
        "b_qkv": np.concatenate([bq[order], bk, bv])[None],
        "w_oT": np.asarray(inputs["L0_attn_Wo"]).T,
        "b_o": np.asarray(inputs["L0_attn_bo"])[None],
    }
    x8 = "L0_xattn_"
    get = lambda n: np.asarray(inputs[x8 + n])
    out["ctxT"] = np.asarray(inputs["ctx_2048"]).reshape(NT, D).T
    out["ln_wb"] = np.stack([get("ln_w"), get("ln_b")]).reshape(2, KC, P).transpose(2, 0, 1)
    out["in_scale"] = np.stack([get(f"{n}_in_scale") for n in ("q", "qx", "k", "v")]).reshape(KINDS, KC, P).transpose(2, 0, 1)
    out["w_scale"] = np.stack([get(f"{n}_scale") for n in ("wq", "wqx", "wk", "wv")])[None]
    out["out_scale"] = np.stack([get("proj_in_scale"), get("proj_w_scale")])[None]
    out["smooth"] = get("proj_smooth").reshape(2, XG * XH, XD).transpose(2, 0, 1)
    out["norm_w"] = np.stack([get(f"{n}ln_w") for n in ("q", "qx", "kx", "k")], 1)
    out["norm_b"] = np.stack([get(f"{n}ln_b") for n in ("q", "qx", "kx", "k")], 1)
    kvx = get("w_kv_x")
    parts = [get("wq"), get("wqx"), kvx[:XG * XD], kvx[XG * XD:], get("wk"), get("wv")]
    out["w_pairs"] = np.concatenate([w.reshape(PAIRS, -1, D) for w in parts], 1).transpose(0, 2, 1)
    proj = get("wproj").T.reshape(2, PAIRS, PH, XD, D)
    out["wproj_pairs"] = proj.transpose(1, 0, 2, 3, 4).reshape(PAIRS, 2 * PH, XD, D)
    f8 = "L0_ffn_"
    out["gateT"] = np.asarray(inputs[f8 + "gate_w"]).T
    tiles = []
    for large, chunk in (("Wg", "cWg"), ("Wu", "cWu")):
        for n, count in ((large, NE * EH), (chunk, NCH * CH)):
            w = np.asarray(inputs[f8 + n]).transpose(1, 0, 2).reshape(KC, P, count // P, P)
            tiles.append(w.transpose(2, 1, 0, 3).reshape(count // P, P, KC * P))
    down = [np.asarray(inputs[f8 + n]).reshape(-1, P, D) for n in ("Wd", "cWd")]
    out["w_tiles"] = np.concatenate([np.concatenate([tiles[0], tiles[2], down[0]], 2),
                                     np.concatenate([tiles[1], tiles[3], down[1]], 2)])
    f = np.float32
    inv = f(1.0) / f(10000.0) ** (np.arange(0, HD, 2, dtype=f) / f(HD))
    ang = np.arange(T, dtype=f)[:, None] * inv[None]
    cos, sin = np.cos(ang), np.sin(ang)
    out["rope"] = np.stack([np.concatenate([cos, cos], 1), np.concatenate([-sin, sin], 1)], 1)
    out["ident"] = np.eye(P, dtype=f)
    rows = np.arange(STACK) % (HALF * HD) // HD
    out["gmask"] = (rows[:, None] == np.arange(HALF)[None]).astype(f)
    sel = np.zeros((TILES, 2, 2, NE, P), f)
    for t in range(TILES):
        for i in range(P):
            if t < E_TILES:
                sel[t, 0, :, (t * P + i) // EH, i] = 1
            else:
                c = ((t - E_TILES) * P + i) // CH
                sel[t, 1, :, c * NE // NCH:(c + 1) * NE // NCH, i] = 1
    out["sel_tiles"] = sel.reshape(TILES, P, P)
    return {n: np.ascontiguousarray(v) for n, v in out.items()}


def kernel(**inputs):
    import concourse.bacc as bacc
    from concourse.bass_utils import run_bass_kernel_spmd

    nc = bacc.Bacc("TRN2", target_bir_lowering=False, num_devices=1)
    arrays = layout(inputs)
    args = {n: nc.dram_tensor(n, v.shape, mybir.dt.from_np(v.dtype), kind="ExternalInput").ap() for n, v in arrays.items()}
    args["out"] = nc.dram_tensor("out", (NB, T, D), F32, kind="ExternalOutput").ap()
    program(nc, args)
    return run_bass_kernel_spmd(nc, [arrays], core_ids=[0]).results[0]["out"]
```
